# Optimizing a Trainium2 kernel written in Bass

```python
import numpy as np
import jax
import jax.numpy as jnp

def _softmax(x, axis=-1):
    return jax.nn.softmax(x, axis=axis)

def _gelu(x):
    return jax.nn.gelu(x, approximate=True)

def _silu(x):
    return jax.nn.silu(x)

def _sigmoid(x):
    return jax.nn.sigmoid(x)

def _layernorm(x, axis=-1, eps=1e-05):
    m = jnp.mean(x, axis=axis, keepdims=True)
    v = jnp.var(x, axis=axis, keepdims=True)
    return (x - m) / jnp.sqrt(v + eps)

def _scatter_add(tgt, idx, src, axis=0):
    return tgt.at[idx].add(src)

def _segment_sum(src, seg, n):
    return jax.ops.segment_sum(src, seg, n)
kernel_name = 'mk_gnn_resnorm_d1_gnn_r8_849a8b'

def setup_inputs(seed: int=0):
    np.random.seed(seed)
    _w = jnp.asarray

    def _rec_inputs():
        import jax
        import jax.numpy as jnp
        _gk = jax.random.key(seed)
        x = -0.0005121 + 1.001 * jax.random.normal(jax.random.fold_in(_gk, 1), (12500, 32), jnp.float32)
        src = jax.random.randint(jax.random.fold_in(_gk, 2), (400000,), 0, 12500, jnp.int32)
        dst = jax.random.randint(jax.random.fold_in(_gk, 3), (400000,), 0, 12500, jnp.int32)
        _o = jnp.argsort(dst, stable=True)
        src = src[_o]
        dst = dst[_o]
        edge_attr_32 = -9.77346e-05 + 0.999888 * jax.random.normal(jax.random.fold_in(_gk, 12), (400000, 32), jnp.float32)
        return (x, src, dst, edge_attr_32)
    x, src, dst, edge_attr_32 = _rec_inputs()

    def _L0_gnn_setup():
        import jax, jax.numpy as jnp
        import numpy as np
        N_NODES = 12500
        N_EDGES = 200000
        D = 32
        key = jax.random.key(seed)
        k1, k2, k3, k4, k5 = jax.random.split(key, 5)
        node_inputs = jax.random.normal(k1, (N_NODES, D), dtype=jnp.float32)
        edge_inputs = jax.random.normal(k2, (N_EDGES, D), dtype=jnp.float32)
        src = jax.random.randint(k3, (N_EDGES,), 0, N_NODES, dtype=jnp.int32)
        dst = jax.random.randint(k4, (N_EDGES,), 0, N_NODES, dtype=jnp.int32)
        lim = 1.0 / np.sqrt(D)
        W = jax.random.uniform(k5, (D, D), minval=-lim, maxval=lim, dtype=jnp.float32)
        b = jnp.zeros((D,), dtype=jnp.float32)
        eps = jnp.zeros((1,), dtype=jnp.float32)
        return {'node_inputs': node_inputs, 'edge_inputs': edge_inputs, 'src': src, 'dst': dst, 'W': W, 'b': b, 'eps': eps}
    _L0_gnn_all = _L0_gnn_setup()
    _L0_gnn_in = {k: v for k, v in _L0_gnn_all.items() if k in ('W', 'b', 'eps')}
    del _L0_gnn_all
    return {'x': x, 'src': src, 'dst': dst, 'edge_attr_32': edge_attr_32, 'L0_gnn_W': _L0_gnn_in['W'], 'L0_gnn_b': _L0_gnn_in['b'], 'L0_gnn_eps': _L0_gnn_in['eps']}

def reference(x, src, dst, edge_attr_32, L0_gnn_W, L0_gnn_b, L0_gnn_eps):
    import jax
    import jax.numpy as jnp

    def _L0_gnn_ref(node_inputs, edge_inputs, src, dst, W, b, eps):
        import jax, jax.numpy as jnp
        import numpy as np
        N_NODES = 12500
        N_EDGES = 200000
        D = 32
        msg = jax.nn.relu(node_inputs[src] + edge_inputs)
        agg = jax.ops.segment_sum(msg, dst, num_segments=N_NODES)
        h = (1.0 + eps[0]) * node_inputs + agg
        return h @ W.T + b
    x = _layernorm(x + _L0_gnn_ref(x, edge_attr_32, src, dst, L0_gnn_W, L0_gnn_b, L0_gnn_eps), axis=-1)
    return x

_drawn_inputs = setup_inputs


def setup_inputs(seed=0):
    import zlib

    import numpy as np

    out = dict(_drawn_inputs(seed))
    spreads = {'L0_gnn_b': (0.0, 0.708)}
    factors = {}
    for name, (base, spread) in spreads.items():
        noise = np.random.default_rng([zlib.crc32(name.encode()), seed]).standard_normal(out[name].shape)
        drawn = base * np.exp(spread * noise) if base else spread * noise
        out[name] = jnp.asarray(drawn.astype(out[name].dtype))
    for name, factor in factors.items():
        out[name] = (out[name] * factor).astype(out[name].dtype)
    return out
```

```python
import concourse.bass as bass
from concourse import mybir
from contextlib import ExitStack

P = 128


def gnn_kernel(nc, x, src, dst, edge, weight, bias, eps, out):
    F32, I32 = mybir.dt.float32, mybir.dt.int32
    ALU, ACT, AX = mybir.AluOpType, mybir.ActivationFunctionType, mybir.AxisListType

    NODES, D = x.shape
    EDGES = src.shape[0]
    TILES = 25
    BATCH = P * TILES
    BATCHES = EDGES // BATCH
    RING = 4
    PEEL = RING + (BATCHES - RING) % RING
    ROUNDS = (BATCHES - PEEL) // RING
    WINDOW = 192
    WINDOWS = -(-NODES // WINDOW)
    ROW = TILES * D
    NP = 125
    NT = NODES // NP
    TGROUP = 4
    OGROUP = 10
    OGROUPS = NT // OGROUP
    LN_EPS = 1e-5
    assert EDGES == BATCH * BATCHES and NODES == NP * NT and PEEL + ROUNDS * RING == BATCHES
    assert NT % TGROUP == 0 and NT % OGROUP == 0 and BATCHES <= P

    src_v = src.rearrange("(b p j) -> b p j", p=P, j=TILES)
    dst_v = dst.rearrange("(b p j) -> p b j", p=P, j=TILES)
    dst_rows = dst.rearrange("(b e) -> b e", e=BATCH)
    edge_v = edge.rearrange("(b p j) f -> b p (j f)", p=P, j=TILES)
    x_v = x.rearrange("(p t) f -> p t f", t=NT)
    out_v = out.rearrange("(p t) f -> p t f", t=NT)
    base_dram = nc.dram_tensor("base_dram", [1, BATCHES], F32, kind="Internal").ap()

    ctx = ExitStack()
    with ctx:
        def sb(name, shape, dt=F32):
            return ctx.enter_context(nc.sbuf_tensor(name, shape, dt))

        def ps(name, shape):
            return ctx.enter_context(nc.psum_tensor(name, shape, F32))

        def sem(name):
            return ctx.enter_context(nc.semaphore(name))

        index = [sb(f"index{s}", [P, TILES], I32) for s in range(RING)]
        rows = [sb(f"rows{s}", [P, ROW]) for s in range(RING)]
        msg = [sb(f"msg{s}", [P, ROW]) for s in range(RING)]
        onehot = [sb(f"onehot{s}", [P, TILES, WINDOW]) for s in range(2)]
        win = [ps(f"win{s}", [P, 512]) for s in range(2)]
        PAD = (WINDOWS + 1) * WINDOW
        hT = sb("hT", [2 * D + 1, PAD])
        aggT = hT[0:D, :]
        x_sb = sb("x_sb", [NP, NT, D])
        rel = sb("rel", [P, BATCHES, TILES])
        base_all = sb("base_all", [P, BATCHES])
        base_row = sb("base_row", [1, BATCHES], I32)
        span_row = sb("span_row", [1, BATCHES])
        span_max = sb("span_max", [1, 1], I32)
        dst_sb = sb("dst_sb", [P, BATCHES, TILES], I32)
        dst_b = sb("dst_b", [BATCHES, BATCH], I32)
        dmin = sb("dmin", [BATCHES, 1])
        dmax = sb("dmax", [BATCHES, 1])
        base_i = sb("base_i", [BATCHES, 1], I32)
        span = sb("span", [BATCHES, 1])
        iota_sb = sb("iota_sb", [P, WINDOW], I32)
        lane_i = sb("lane_i", [P, 1], I32)
        lane = sb("lane", [P, 1])
        ident = sb("ident", [P, P])
        eps_sb = sb("eps_sb", [D, 1])
        scale = sb("scale", [D, 1])
        w_sb = sb("w_sb", [D, D])
        wb = sb("wb", [2 * D + 1, D])
        wmean = sb("wmean", [2 * D + 1, 1])
        far = sb("far", [P, TILES])
        lneps = sb("lneps", [NP, 1])
        passes_done = sb("passes_done", [1, 1])
        iota = ps("iota", [P, 512])
        xT = [ps(f"xT{s}", [P, 512]) for s in range(2)]
        z = [ps(f"z{s}", [P, 512]) for s in range(2)]
        var = sb("var", [NP, NT])
        rstd = sb("rstd", [NP, NT])
        y_sb = x_sb
        sq = [sb(f"sq{s}", [NP, OGROUP, D]) for s in range(2)]

        index_loaded = [sem(f"index_loaded{s}") for s in range(RING)]
        edges_loaded = [sem(f"edges_loaded{s}") for s in range(RING)]
        rows_gathered = [sem(f"rows_gathered{s}") for s in range(RING)]
        sums_ready = sem("sums_ready")
        msgs_ready = sem("msgs_ready")
        onehot_ready = sem("onehot_ready")
        win_ready = sem("win_ready")
        win_added = sem("win_added")
        dst_loaded = sem("dst_loaded")
        x_loaded = sem("x_loaded")
        small_loaded = sem("small_loaded")
        bases_ready = sem("bases_ready")
        base_written = sem("base_written")
        base_rows_loaded = sem("base_rows_loaded")
        base_all_loaded = sem("base_all_loaded")
        gathers_started = sem("gathers_started")
        iota_ready = sem("iota_ready")
        ident_ready = sem("ident_ready")
        setup_step = sem("setup_step")
        wT_ready = sem("wT_ready")
        wb_ready = sem("wb_ready")
        bias_loaded = sem("bias_loaded")
        xT_ready = sem("xT_ready")
        scale_ready = sem("scale_ready")
        rel_ready = sem("rel_ready")
        span_ready = sem("span_ready")
        h_started = sem("h_started")
        x_copied = sem("x_copied")
        agg_ready = sem("agg_ready")
        z_ready = sem("z_ready")
        ln_step = sem("ln_step")
        sq_ready = sem("sq_ready")
        var_ready = sem("var_ready")
        std_ready = sem("std_ready")
        out_ready = sem("out_ready")
        out_stored = sem("out_stored")
        far_loaded = sem("far_loaded")
        far_gathered = sem("far_gathered")
        far_sums = sem("far_sums")
        far_msgs = sem("far_msgs")
        far_step = sem("far_step")
        far_onehot = sem("far_onehot")
        far_win = sem("far_win")
        far_added = sem("far_added")

        block = ctx.enter_context(nc.Block())

        def batches(eng, step):
            for b in range(PEEL):
                step(b, b % RING, b // RING)
            with eng.Fori(0, ROUNDS) as i:
                for u in range(RING):
                    step(i * RING + (PEEL + u), (PEEL + u) % RING, i + (PEEL + u) // RING)

        h_v = hT[:, 0:NODES].rearrange("f (p t) -> f t p", t=NT)

        def xT_group(g):
            return xT[g % 2][0:D, 0:TGROUP * NP].rearrange("f (t p) -> f t p", p=NP)

        def z_group(g):
            return z[g % 2][0:NP, 0:OGROUP * D].rearrange("p (t f) -> p t f", f=D)

        def one(ap3, b):
            return ap3[bass.ds(b, 1), :, :].rearrange("o p f -> (o p) f")

        @block.sync
        def _(sp):
            sp.dma_start(index[0][:, :], src_v[0]).then_inc(index_loaded[0], 16)
            sp.dma_start(dst_b[:, :], dst_rows).then_inc(dst_loaded, 16)
            sp.dma_start(x_sb[:, :, :], x_v).then_inc(x_loaded, 16)
            sp.dma_start(w_sb[:, :], weight).then_inc(small_loaded, 16)
            sp.dma_start(eps_sb[:, :], eps.rearrange("(a b) -> a b", a=1).to_broadcast([D, 1])).then_inc(small_loaded, 16)
            sp.dma_start(wb[2 * D:2 * D + 1, :], bias.rearrange("(a f) -> a f", a=1)).then_inc(bias_loaded, 16)

            def load(b, slot, use):
                first = isinstance(use, int) and use == 0
                if not first:
                    sp.wait_ge(rows_gathered[slot], use * (16 * TILES))
                if not (first and slot == 0):
                    sp.dma_start(index[slot][:, :], one(src_v, b)).then_inc(index_loaded[slot], 16)
                if not first:
                    sp.wait_ge(win_ready, b - RING + 1)
                sp.dma_start(msg[slot][:, :], one(edge_v, b)).then_inc(edges_loaded[slot], 16)

            batches(sp, load)

            sp.wait_ge(span_ready, 1)
            reach = sp.value_load(span_max[0:1, 0:1], min_val=0, max_val=NODES)
            with sp.If(reach >= WINDOW):
                with sp.Fori(0, BATCHES) as b:
                    sp.wait_ge(far_added, b * WINDOWS + 1)
                    sp.dma_start(index[0][:, :], one(src_v, b)).then_inc(far_loaded, 16)
                    sp.dma_start(msg[0][:, :], one(edge_v, b)).then_inc(far_loaded, 16)

            for g in range(OGROUPS):
                t = slice(g * OGROUP, (g + 1) * OGROUP)
                sp.wait_ge(out_ready, g + 1)
                sp.dma_start(out_v[:, t, :], y_sb[:, t, :]).then_inc(out_stored, 16)
            sp.wait_ge(out_stored, 16 * OGROUPS)

        @block.gpsimd
        def _(pool):
            nc.gpsimd.iota(iota_sb[:, :], pattern=[[1, WINDOW]], base=0, channel_multiplier=0).then_inc(iota_ready, 1)
            nc.gpsimd.iota(lane_i[:, :], pattern=[[0, 1]], base=0, channel_multiplier=1).then_inc(iota_ready, 1)

            def gather_tiles(slot, done):
                pool.sem_inc(gathers_started, 1)
                for j in range(TILES):
                    pool.indirect_dma_start(
                        rows[slot][:, j * D:(j + 1) * D], None, x,
                        bass.IndirectOffsetOnAxis(index[slot][:, j:j + 1], 0)).then_inc(done, 16)

            def gather(b, slot, use):
                if not (isinstance(use, int) and use == 0):
                    pool.wait_ge(sums_ready, b - RING + 1)
                pool.wait_ge(index_loaded[slot], use * 16 + 16)
                gather_tiles(slot, rows_gathered[slot])

            batches(pool, gather)

            pool.wait_ge(span_ready, 1)
            reach = pool.value_load(span_max[0:1, 0:1], min_val=0, max_val=NODES)
            with pool.If(reach >= WINDOW):
                with pool.Fori(0, BATCHES) as b:
                    pool.wait_ge(far_loaded, b * 32 + 32)
                    gather_tiles(0, far_gathered)

        @block.vector
        def _(dve):
            steps = [0]

            def wait_own(ins):
                steps[0] += 1
                ins.then_inc(setup_step, 1)
                dve.wait_ge(setup_step, steps[0])

            dve.wait_ge(dst_loaded, 16)
            nc.vector.tensor_reduce(dmin[:, :], dst_b[:, :], AX.X, ALU.min)
            wait_own(nc.vector.tensor_reduce(dmax[:, :], dst_b[:, :], AX.X, ALU.max))
            nc.vector.tensor_copy(base_i[:, :], dmin[:, :])
            nc.vector.tensor_tensor(span[:, :], dmax[:, :], dmin[:, :], ALU.subtract).then_inc(bases_ready, 1)
            dve.wait_ge(iota_ready, 2)
            wait_own(nc.vector.tensor_copy(lane[:, :], lane_i[:, :]))
            nc.vector.tensor_copy(iota[:, 0:WINDOW], iota_sb[:, :])
            nc.vector.tensor_scalar(ident[:, :], iota_sb[:, 0:P], lane[:, 0:1], None, ALU.is_equal).then_inc(ident_ready, 1)
            nc.vector.memset(lneps[:, :], LN_EPS)
            nc.vector.memset(hT[2 * D:2 * D + 1, :], 1.0)
            wait_own(nc.vector.memset(hT[0:D, NODES:PAD], 0.0))
            dve.wait_ge(base_all_loaded, 32)
            nc.vector.tensor_tensor(rel[:, :, :], dst_sb[:, :, :],
                                    base_all[:, :].rearrange("p (b o) -> p b o", o=1).to_broadcast([P, BATCHES, TILES]),
                                    ALU.subtract).then_inc(rel_ready, 1)
            dve.wait_ge(base_rows_loaded, 32)
            nc.vector.tensor_reduce(span_max[0:1, 0:1], span_row[0:1, :], AX.X, ALU.max).then_inc(span_ready, 1)
            dve.wait_ge(small_loaded, 32)
            wait_own(nc.vector.tensor_scalar(scale[:, :], eps_sb[:, :], 1.0, None, ALU.add))
            dve.wait_ge(x_copied, NT // TGROUP)
            nc.vector.tensor_scalar(aggT[:, 0:NODES], hT[D:2 * D, 0:NODES], scale[:, 0:1], None, ALU.mult).then_inc(h_started, 1)
            dve.wait_ge(wT_ready, 1)
            dve.wait_ge(bias_loaded, 16)
            nc.vector.tensor_reduce(wmean[0:D, :], z[0][0:D, 0:D], AX.X, ALU.add)
            wait_own(nc.vector.tensor_reduce(wmean[2 * D:2 * D + 1, :], wb[2 * D:2 * D + 1, :], AX.X, ALU.add))
            nc.vector.tensor_scalar(wmean[0:D, :], wmean[0:D, :], 1.0 / D, None, ALU.mult)
            wait_own(nc.vector.tensor_scalar(wmean[2 * D:2 * D + 1, :], wmean[2 * D:2 * D + 1, :], 1.0 / D, None, ALU.mult))
            nc.vector.tensor_scalar(wb[0:D, :], z[0][0:D, 0:D], wmean[0:D, 0:1], None, ALU.subtract)
            nc.vector.tensor_scalar(wb[D:2 * D, :], ident[D:2 * D, D:2 * D], 1.0 / D, None, ALU.subtract)
            nc.vector.tensor_scalar(wb[2 * D:2 * D + 1, :], wb[2 * D:2 * D + 1, :], wmean[2 * D:2 * D + 1, 0:1], None,
                                    ALU.subtract).then_inc(wb_ready, 1)
            dve.wait_ge(h_started, 1)
            dve.wait_ge(rel_ready, 1)

            def mark(slot2, which):
                return nc.vector.tensor_tensor(
                    onehot[slot2][:, :, :],
                    iota[:, 0:WINDOW].rearrange("p (o w) -> p o w", o=1).to_broadcast([P, TILES, WINDOW]),
                    which.to_broadcast([P, TILES, WINDOW]), ALU.is_equal)

            def add_window(b, slot2):
                base = dve.value_load(base_row[0:1, bass.ds(b, 1)], min_val=0, max_val=NODES - 1)
                dve.wait_ge(win_ready, b + 1)
                if not (isinstance(b, int) and b == 0):
                    dve.wait_ge(win_added, b)
                at = aggT[0:D, bass.ds(base, WINDOW)]
                nc.vector.tensor_tensor(at, at, win[slot2][0:D, 0:WINDOW], ALU.add).then_inc(win_added, 1)

            def batch(b, slot, use):
                first = isinstance(use, int) and use == 0
                slot2 = slot % 2
                if not (first and slot < 2):
                    dve.wait_ge(win_ready, b - 1)
                which = rel[:, bass.ds(b, 1), :].rearrange("p o j -> p (o j)").rearrange("p (j o) -> p j o", o=1)
                mark(slot2, which).then_inc(onehot_ready, 1)
                dve.wait_ge(rows_gathered[slot], use * (16 * TILES) + 16 * TILES)
                dve.wait_ge(edges_loaded[slot], use * 16 + 16)
                nc.vector.tensor_tensor(msg[slot][:, :], rows[slot][:, :], msg[slot][:, :], ALU.add).then_inc(sums_ready, 1)
                if not (first and slot == 0):
                    add_window(b - 1, (slot - 1) % 2)

            dve.wait_ge(base_rows_loaded, 32)
            batches(dve, batch)
            add_window(BATCHES - 1, (BATCHES - 1) % 2)

            dve.wait_ge(span_ready, 1)
            reach = dve.value_load(span_max[0:1, 0:1], min_val=0, max_val=NODES)
            dve.wait_ge(win_added, BATCHES)
            with dve.If(reach >= WINDOW):
                nc.vector.memset(far[:, :], 0.0).then_inc(far_added, 1)
                with dve.Fori(0, BATCHES) as b:
                    relb = rel[:, bass.ds(b, 1), :].rearrange("p o j -> p (o j)")
                    dve.wait_ge(far_gathered, b * (16 * TILES) + 16 * TILES)
                    dve.wait_ge(far_loaded, b * 32 + 32)
                    nc.vector.tensor_tensor(msg[0][:, :], rows[0][:, :], msg[0][:, :], ALU.add).then_inc(far_sums, 1)
                    nc.vector.tensor_scalar(far[:, :], relb, base_all[:, bass.ds(b, 1)], 1.0, ALU.add, ALU.add).then_inc(far_step, 1)
                    dve.wait_ge(far_step, b * (WINDOWS + 3) + 1)
                    nc.vector.scalar_tensor_tensor(far[:, :], relb, float(WINDOW), far[:, :], ALU.is_ge, ALU.mult).then_inc(far_step, 1)
                    dve.wait_ge(far_step, b * (WINDOWS + 3) + 2)
                    nc.vector.tensor_scalar(far[:, :], far[:, :], 1.0, None, ALU.subtract).then_inc(far_step, 1)
                    with dve.Fori(0, WINDOWS) as w:
                        dve.wait_ge(far_step, b * (WINDOWS + 3) + w + 3)
                        mark(0, far[:, :].rearrange("p (j o) -> p j o", o=1)).then_inc(far_onehot, 1)
                        dve.wait_ge(far_onehot, b * WINDOWS + w + 1)
                        nc.vector.tensor_scalar(far[:, :], far[:, :], float(WINDOW), None, ALU.subtract).then_inc(far_step, 1)
                        dve.wait_ge(far_win, b * WINDOWS + w + 1)
                        at = aggT[0:D, bass.ds(w * WINDOW, WINDOW)]
                        nc.vector.tensor_tensor(at, at, win[0][0:D, 0:WINDOW], ALU.add).then_inc(far_added, 1)

                dve.wait_ge(far_added, BATCHES * WINDOWS + 1)
            nc.vector.memset(passes_done[:, :], 0.0).then_inc(agg_ready, 1)

            for g in range(OGROUPS):
                t = slice(g * OGROUP, (g + 1) * OGROUP)
                dve.wait_ge(sq_ready, g + 1)
                nc.vector.tensor_reduce(var[:, t], sq[g % 2][:, :, :], AX.X, ALU.add).then_inc(var_ready, 1)
                dve.wait_ge(std_ready, g + 1)
                nc.vector.reciprocal(rstd[:, t], rstd[:, t]).then_inc(ln_step, 1)
                dve.wait_ge(ln_step, g + 1)
                nc.vector.tensor_tensor(y_sb[:, t, :], z_group(g),
                                        rstd[:, t].rearrange("p (t o) -> p t o", o=1).to_broadcast([NP, OGROUP, D]),
                                        ALU.mult).then_inc(out_ready, 1)

        @block.scalar
        def _(act):
            act.dma_start(dst_sb[:, :, :], dst_v).then_inc(base_all_loaded, 16)
            act.wait_ge(bases_ready, 1)
            act.dma_start(base_dram.rearrange("o b -> b o"), dmin[:, :]).then_inc(base_written, 16)
            act.dma_start(base_row[0:1, :], base_i[:, :]).then_inc(base_rows_loaded, 16)
            act.dma_start(span_row[0:1, :], span[:, :]).then_inc(base_rows_loaded, 16)
            act.wait_ge(base_written, 16)
            act.dma_start(base_all[:, :], base_dram.to_broadcast([P, BATCHES])).then_inc(base_all_loaded, 16)

            for g in range(NT // TGROUP):
                act.wait_ge(xT_ready, g + 1)
                nc.scalar.copy(h_v[D:2 * D, g * TGROUP:(g + 1) * TGROUP, :], xT_group(g)).then_inc(x_copied, 1)

            def relu(b, slot, use):
                act.wait_ge(sums_ready, b + 1)
                nc.scalar.activation(msg[slot][:, :], msg[slot][:, :], ACT.Relu).then_inc(msgs_ready, 1)

            batches(act, relu)

            act.wait_ge(span_ready, 1)
            reach = act.value_load(span_max[0:1, 0:1], min_val=0, max_val=NODES)
            with act.If(reach >= WINDOW):
                with act.Fori(0, BATCHES) as b:
                    act.wait_ge(far_sums, b + 1)
                    nc.scalar.activation(msg[0][:, :], msg[0][:, :], ACT.Relu).then_inc(far_msgs, 1)

            for g in range(OGROUPS):
                t = slice(g * OGROUP, (g + 1) * OGROUP)
                act.wait_ge(z_ready, g + 1)
                if g >= 2:
                    act.wait_ge(var_ready, g - 1)
                nc.scalar.activation(sq[g % 2][:, :, :], z_group(g), ACT.Square).then_inc(sq_ready, 1)
                act.wait_ge(var_ready, g + 1)
                nc.scalar.activation(rstd[:, t], var[:, t], ACT.Sqrt, bias=lneps[:, 0:1], scale=1.0 / D).then_inc(std_ready, 1)

        @block.tensor
        def _(pe):
            pe.wait_ge(ident_ready, 1)
            pe.wait_ge(small_loaded, 32)
            nc.tensor.transpose(z[0][0:D, 0:D], w_sb[:, :], ident[0:D, 0:D]).then_inc(wT_ready, 1)
            pe.wait_ge(x_loaded, 16)

            for g in range(NT // TGROUP):
                if g >= 2:
                    pe.wait_ge(x_copied, g - 1)
                for t in range(TGROUP):
                    last = nc.tensor.transpose(xT[g % 2][0:D, t * NP:(t + 1) * NP], x_sb[:, g * TGROUP + t, :],
                                               ident[0:NP, 0:NP])
                last.then_inc(xT_ready, 1)

            def sum_tiles(slot, slot2):
                for j in range(TILES):
                    last = nc.tensor.matmul(win[slot2][0:D, 0:WINDOW], msg[slot][:, j * D:(j + 1) * D],
                                            onehot[slot2][:, j, :], start=(j == 0), stop=(j == TILES - 1))
                return last

            def batch(b, slot, use):
                if not (isinstance(use, int) and use == 0 and slot < 2):
                    pe.wait_ge(win_added, b - 1)
                pe.wait_ge(onehot_ready, b + 1)
                pe.wait_ge(msgs_ready, b + 1)
                sum_tiles(slot, slot % 2).then_inc(win_ready, 1)

            batches(pe, batch)

            pe.wait_ge(span_ready, 1)
            reach = pe.value_load(span_max[0:1, 0:1], min_val=0, max_val=NODES)
            with pe.If(reach >= WINDOW):
                with pe.Fori(0, BATCHES) as b:
                    with pe.Fori(0, WINDOWS) as w:
                        pe.wait_ge(far_msgs, b + 1)
                        pe.wait_ge(far_added, b * WINDOWS + w + 1)
                        pe.wait_ge(far_onehot, b * WINDOWS + w + 1)
                        sum_tiles(0, 0).then_inc(far_win, 1)

            pe.wait_ge(wb_ready, 1)
            pe.wait_ge(x_copied, NT // TGROUP)
            pe.wait_ge(agg_ready, 1)
            for g in range(OGROUPS):
                if g >= 2:
                    pe.wait_ge(out_ready, g - 1)
                for t in range(OGROUP):
                    last = nc.tensor.matmul(z[g % 2][0:NP, t * D:(t + 1) * D], h_v[:, g * OGROUP + t, :], wb[:, :], start=True, stop=True)
                last.then_inc(z_ready, 1)


def kernel(x, src, dst, edge_attr_32, L0_gnn_W, L0_gnn_b, L0_gnn_eps):
    import numpy as np
    import concourse.bacc as bacc
    from concourse import mybir as mb
    from concourse.bass_utils import run_bass_kernel_spmd

    given = {"x": x, "src": src, "dst": dst, "edge": edge_attr_32, "weight": L0_gnn_W, "bias": L0_gnn_b, "eps": L0_gnn_eps}
    arrays = {f"in_{n}": np.ascontiguousarray(a) for n, a in given.items()}
    nc = bacc.Bacc("TRN2", target_bir_lowering=False, num_devices=1)
    args = [nc.dram_tensor(n, a.shape, mb.dt.from_np(a.dtype), kind="ExternalInput").ap() for n, a in arrays.items()]
    out = nc.dram_tensor("out", list(x.shape), mb.dt.float32, kind="ExternalOutput").ap()
    gnn_kernel(nc, *args, out)
    r = run_bass_kernel_spmd(nc, [arrays], core_ids=[0])
    return r.results[0]["out"]
```

```python
import concourse.bass as bass
from concourse import mybir
from collections import namedtuple
from contextlib import ExitStack

Step = namedtuple("Step", "b slot use first last looks looks_on turns")

P = 128
PARTS = 3
FEATURES = 3


def gnn_kernel(nc, x, src, dst, edge, weight, bias, eps, out):
    F32, I32, BF16 = mybir.dt.float32, mybir.dt.int32, mybir.dt.bfloat16
    ALU, ACT, AX = mybir.AluOpType, mybir.ActivationFunctionType, mybir.AxisListType

    NODES, D = x.shape
    EDGES = src.shape[0]
    TILES = 25
    BATCH = P * TILES
    BATCHES = EDGES // BATCH
    RING = 4
    PEEL, LAST = RING + 1, RING
    ROUNDS = (BATCHES - PEEL - LAST) // RING
    ROW = TILES * D
    LOOK = 4
    POOLED = TILES - LOOK
    COLS = P * LOOK
    SIDE = P // D
    BLOCK = P * SIDE
    BLOCKS = -(-NODES // BLOCK)
    FULL = NODES // BLOCK
    REST = (NODES - FULL * BLOCK) // SIDE
    BY_ACT = 12
    BY_DVE = BLOCKS - BY_ACT
    AHEAD = 3
    WINDOW = 128
    WINDOWS = -(-NODES // WINDOW)
    PAD = (WINDOWS + 1) * WINDOW
    SUMS = PARTS * D
    MARK = 5
    MARKS = TILES // MARK
    SUM_EVERY, SIDE_AT, BACK_AT, SRC_AT = BLOCKS // MARKS, 6, 10, 18
    HIGH_AT, MID_AT, COPY_AT = 2, 7, 5
    MARK_AT, REST_AT, WINDOW_AT, LOW_AT = (3, 4, 6, 8, 9), 5, 7, 11
    NP = 125
    NT = NODES // NP
    TGROUP = 4
    OGROUP = 4
    ROUNDS_OUT = [(t, min(OGROUP, (NT - t) // SIDE)) for t in range(0, NT, OGROUP * SIDE)]
    LN_EPS = 1e-5
    assert EDGES == BATCH * BATCHES and PEEL + ROUNDS * RING + LAST == BATCHES and BATCHES <= P
    assert NODES == NP * NT and NT % TGROUP == 0 and NT % SIDE == 0 and SUMS + D == P
    assert TILES % MARK == 0 and BLOCKS % MARKS == 0 and NODES % SIDE == 0 and BATCHES % 2 == 1

    by_act = [(i + 1) * BY_ACT // BLOCKS > i * BY_ACT // BLOCKS for i in range(BLOCKS)]
    act_blocks = [i for i in range(BLOCKS) if by_act[i]]
    dve_blocks = [i for i in range(BLOCKS) if not by_act[i]]

    src_v = src.rearrange("(b p j) -> b p j", p=P, j=TILES)
    src_rows = src.rearrange("(b e) -> b e", e=BATCH)
    dst_v = dst.rearrange("(b p j) -> p b j", p=P, j=TILES)
    dst_rows = dst.rearrange("(b e) -> b e", e=BATCH)
    edge_v = edge.rearrange("(b p j) f -> b p (j f)", p=P, j=TILES)
    x_v = x.rearrange("(p t) f -> p t f", t=NT)
    x_blocks = x[0:FULL * BLOCK, :].rearrange("(b p s) f -> p b (s f)", p=P, s=SIDE)
    x_rest = x[FULL * BLOCK:, :].rearrange("(p s) f -> p (s f)", s=SIDE)
    out_v = out.rearrange("(p t) f -> p t f", t=NT)
    base_dram = nc.dram_tensor("base_dram", [1, BATCHES], F32, kind="Internal").ap()
    feat_dram = nc.dram_tensor("feat_dram", [BATCHES - 1, FEATURES, COLS], BF16, kind="Internal").ap()

    ctx = ExitStack()
    with ctx:
        def sb(name, shape, dt=F32):
            return ctx.enter_context(nc.sbuf_tensor(name, shape, dt))

        def ps(name):
            return ctx.enter_context(nc.psum_tensor(name, [P, 512], F32))

        def sem(name):
            return ctx.enter_context(nc.semaphore(name))

        index = [sb(f"index{s}", [P, TILES], I32) for s in range(RING)]
        rows = [sb(f"rows{s}", [P, ROW]) for s in range(RING)]
        msg = [sb(f"msg{s}", [P, ROW]) for s in range(RING)]
        msg_parts = [sb(f"msg_parts{s}", [P, TILES, PARTS, D], BF16) for s in range(2)]
        onehots = sb("onehots", [P, 2, TILES, WINDOW], BF16)
        onehot = [onehots[:, s, :, :] for s in range(2)]
        win = [ps(f"win{s}") for s in range(2)]
        parts = sb("parts", [P, BLOCKS, PARTS, P], BF16)
        keys = sb("keys", [P, BLOCKS])
        minus_keys = sb("minus_keys", [P, BLOCKS])
        feat = [sb(f"feat{s}", [P, COLS], BF16) for s in range(2)]
        spread = sb("spread", [P, 2, P], BF16)
        look = sb("look", [P, BLOCKS, COLS], BF16)
        side_of = sb("side_of", [P, 1])
        side_sb = sb("side_sb", [P, COLS])
        picked_sb = sb("picked_sb", [P, COLS])
        fold = sb("fold", [P, D])
        key_sb = sb("key_sb", [P, COLS])
        src_ps = [ps(f"src_ps{s}") for s in range(2)]
        act_ps = ps("act_ps")
        found_ps = ps("found_ps")
        back_ps = ps("back_ps")
        aggX = sb("aggX", [P, PAD])
        x_sb = sb("x_sb", [NP, NT, D])
        rel = sb("rel", [P, BATCHES, TILES])
        dst_sb = rel[:, :, :].bitcast(I32)
        base_all = sb("base_all", [P, BATCHES])
        base_row = sb("base_row", [1, BATCHES], I32)
        span_row = sb("span_row", [1, BATCHES])
        span_max = sb("span_max", [1, 1], I32)
        wb = sb("wb", [P, D])
        bias_row = sb("bias_row", [1, SIDE, D])
        bias_col = sb("bias_col", [P, 1])
        one_one = sb("one_one", [1, 1])
        x_stage = sb("x_stage", [P, BLOCKS, P])
        zeros = sb("zeros", [P, 1])
        dst_b = onehots[0:BATCHES, :, :, :].rearrange("p s j w -> p (s j w)").bitcast(I32)
        src_b = look[0:BATCHES - 1, :, :].rearrange("p b c -> p (b c)").bitcast(I32)[:, 0:BATCH]
        hi_i, lo_i, side_i = (msg[s][0:BATCHES - 1, 0:COLS].bitcast(I32) for s in (1, 2, 3))
        dmin = sb("dmin", [BATCHES, 1])
        dmax = sb("dmax", [BATCHES, 1])
        base_i = sb("base_i", [BATCHES, 1], I32)
        span = sb("span", [BATCHES, 1])
        feat_all = sb("feat_all", [BATCHES - 1, FEATURES, COLS], BF16)
        keys_i = sb("keys_i", [P, BLOCKS], I32)
        side_of_i = sb("side_of_i", [P, 1], I32)
        key_rows = sb("key_rows", [P, 1])
        iota_sb = sb("iota_sb", [P, WINDOW], I32)
        lane_i = sb("lane_i", [P, 1], I32)
        lane = sb("lane", [P, 1])
        ident = sb("ident", [P, P])
        scale = sb("scale", [P, 1])
        w_rep = sb("w_rep", [D, P])
        w_mean = sb("w_mean", [P, 1])
        ident_c = sb("ident_c", [P, D])
        bias_mean = sb("bias_mean", [1, 1])
        far = sb("far", [P, TILES])
        passes_done = sb("passes_done", [1, 1])
        lneps = sb("lneps", [NP, 1])
        iota = ps("iota")
        xT = win
        zT = src_ps
        z = [found_ps, back_ps]
        y_sb = x_sb
        var = sb("var", [NP, NT])
        rstd = sb("rstd", [NP, NT])
        zT_sb = [rows[s] for s in range(2)]
        sq = [msg[s] for s in range(2)]

        index_loaded = [sem(f"index_loaded{s}") for s in range(RING)]
        edges_loaded = [sem(f"edges_loaded{s}") for s in range(RING)]
        rows_gathered = [sem(f"rows_gathered{s}") for s in range(RING)]
        first_gathered = sem("first_gathered")
        gathers_started = sem("gathers_started")
        sums_ready = sem("sums_ready")
        sums_step = sem("sums_step")
        high_ready = sem("high_ready")
        rest_ready = sem("rest_ready")
        mid_ready = sem("mid_ready")
        msgs_ready = sem("msgs_ready")
        onehot_ready = sem("onehot_ready")
        win_ready = sem("win_ready")
        win_added = sem("win_added")
        feat_loaded = [sem(f"feat_loaded{s}") for s in range(2)]
        src_ready = sem("src_ready")
        keys_ready = sem("keys_ready")
        keys_copied = sem("keys_copied")
        side_ready = sem("side_ready")
        squared = sem("squared")
        look_act_ready = sem("look_act_ready")
        look_dve_ready = sem("look_dve_ready")
        look_used = sem("look_used")
        side_copied = sem("side_copied")
        picked = sem("picked")
        back_ready = sem("back_ready")
        dst_loaded = sem("dst_loaded")
        src_loaded = sem("src_loaded")
        x_loaded = sem("x_loaded")
        zeros_ready = sem("zeros_ready")
        aggX_cleared = sem("aggX_cleared")
        stage_cleared = sem("stage_cleared")
        bias_ready = sem("bias_ready")
        stage_loaded = sem("stage_loaded")
        weights_loaded = sem("weights_loaded")
        small_loaded = sem("small_loaded")
        spread_ready = sem("spread_ready")
        parts_ready = sem("parts_ready")
        feat_ready = sem("feat_ready")
        feat_written = sem("feat_written")
        bases_ready = sem("bases_ready")
        base_written = sem("base_written")
        base_rows_loaded = sem("base_rows_loaded")
        base_all_loaded = sem("base_all_loaded")
        iota_ready = sem("iota_ready")
        ident_ready = sem("ident_ready")
        setup_step = sem("setup_step")
        w_ready = sem("w_ready")
        wb_ready = sem("wb_ready")
        xT_ready = sem("xT_ready")
        x_copied = sem("x_copied")
        span_ready = sem("span_ready")
        agg_ready = sem("agg_ready")
        zT_ready = sem("zT_ready")
        zT_copied = sem("zT_copied")
        z_ready = sem("z_ready")
        sq_ready = sem("sq_ready")
        var_ready = sem("var_ready")
        std_ready = sem("std_ready")
        rstd_ready = sem("rstd_ready")
        out_ready = sem("out_ready")
        out_stored = sem("out_stored")
        far_loaded = sem("far_loaded")
        far_gathered = sem("far_gathered")
        far_sums = sem("far_sums")
        far_high = sem("far_high")
        far_rest = sem("far_rest")
        far_mid = sem("far_mid")
        far_msgs = sem("far_msgs")
        far_step = sem("far_step")
        far_onehot = sem("far_onehot")
        far_win = sem("far_win")
        far_added = sem("far_added")

        block = ctx.enter_context(nc.Block())

        def batches(eng, step):
            def at(b, rounds):
                step(Step(b=rounds * RING + b, slot=b % RING, use=rounds + b // RING, first=b < RING, last=b == BATCHES - 1,
                          looks=b < BATCHES - 1, looks_on=b < BATCHES - 2, turns=rounds * (RING // 2) + b // 2))

            for b in range(PEEL):
                at(b, 0)
            with eng.Fori(0, ROUNDS) as i:
                for u in range(RING):
                    at(PEEL + u, i)
            for b in range(BATCHES - LAST, BATCHES):
                at(b, 0)

        def reaches(s, n):
            return not s.first or s.slot >= n

        def wait_count(eng, semaphore, count):
            if not (isinstance(count, int) and count <= 0):
                eng.wait_ge(semaphore, count)

        aggX_v = aggX[:, 0:NODES].rearrange("f (p t) -> f t p", t=NT)

        def xT_group(g):
            return xT[g % 2][0:D, 0:TGROUP * NP].rearrange("f (t p) -> f t p", p=NP)

        def z_round(v, per):
            return v.rearrange("p (i r f) -> p i r f", i=per, f=D)

        def z_of(k):
            return z[k % 2][0:NP, 0:ROUNDS_OUT[k][1] * P]

        def sq_of(k):
            return sq[k % 2][0:NP, 0:ROUNDS_OUT[k][1] * P]

        def one(ap3, b):
            return ap3[bass.ds(b, 1), :, :].rearrange("o p f -> (o p) f")

        def feat_of(k):
            return feat_dram[bass.ds(k, 1), :, :].rearrange("o r c -> (o r) c")

        @block.sync
        def _(sp):
            for b in range(RING):
                sp.dma_start(index[b][:, :], src_v[b]).then_inc(index_loaded[b], 16)
            k = (BATCHES - 1) // 16 * 16
            sp.dma_start(src_b[0:k, :], src_rows[1:1 + k, :]).then_inc(src_loaded, 16)
            sp.dma_start(src_b[k:, :], src_rows[1 + k:, :]).then_inc(src_loaded, 16)
            sp.wait_ge(stage_cleared, 1)
            sp.dma_start(x_stage[:, 0:FULL, :], x_blocks).then_inc(stage_loaded, 16)
            sp.dma_start(x_stage[0:REST, FULL, :], x_rest).then_inc(stage_loaded, 16)
            sp.wait_ge(feat_ready, 1)
            sp.dma_start(feat_dram, feat_all[:, :, :]).then_inc(feat_written, 16)
            sp.wait_ge(feat_written, 16)
            sp.dma_start(feat[0][0:FEATURES, :], feat_of(0)).then_inc(feat_loaded[0], 16)
            sp.wait_ge(bases_ready, 1)
            sp.dma_start(base_dram.rearrange("o b -> b o"), dmin[:, :]).then_inc(base_written, 16)
            sp.dma_start(base_row[0:1, :], base_i[:, :]).then_inc(base_rows_loaded, 16)
            sp.dma_start(span_row[0:1, :], span[:, :]).then_inc(base_rows_loaded, 16)
            sp.wait_ge(base_written, 16)
            sp.dma_start(base_all[:, :], base_dram.to_broadcast([P, BATCHES])).then_inc(base_all_loaded, 16)

            def load(s):
                if not s.first:
                    sp.wait_ge(rows_gathered[s.slot], s.use * (16 * POOLED))
                    sp.dma_start(index[s.slot][:, :], one(src_v, s.b)).then_inc(index_loaded[s.slot], 16)
                if not s.first:
                    sp.wait_ge(msgs_ready, s.b - RING + 1)
                sp.dma_start(msg[s.slot][:, :], one(edge_v, s.b)).then_inc(edges_loaded[s.slot], 16)
                if s.looks and not (s.first and s.slot == 0):
                    wait_count(sp, side_ready, s.b - 1)
                    sp.dma_start(feat[s.slot % 2][0:FEATURES, :], feat_of(s.b)).then_inc(feat_loaded[s.slot % 2], 16)

            batches(sp, load)

            sp.wait_ge(span_ready, 1)
            reach = sp.value_load(span_max[0:1, 0:1], min_val=0, max_val=NODES)
            with sp.If(reach >= WINDOW):
                with sp.Fori(0, BATCHES) as b:
                    sp.wait_ge(far_added, b * WINDOWS + 1)
                    sp.dma_start(index[0][:, :], one(src_v, b)).then_inc(far_loaded, 16)
                    sp.dma_start(msg[0][:, :], one(edge_v, b)).then_inc(far_loaded, 16)

            for k, (t0, per) in enumerate(ROUNDS_OUT):
                t = slice(t0, t0 + per * SIDE)
                sp.wait_ge(out_ready, k + 1)
                sp.dma_start(out_v[:, t, :], y_sb[:, t, :]).then_inc(out_stored, 16)
            sp.wait_ge(out_stored, 16 * len(ROUNDS_OUT))

        @block.gpsimd
        def _(pool):
            nc.gpsimd.iota(iota_sb[:, :], pattern=[[1, WINDOW]], base=0, channel_multiplier=0).then_inc(iota_ready, 1)
            nc.gpsimd.iota(keys_i[:, :], pattern=[[P, BLOCKS]], base=0, channel_multiplier=1).then_inc(iota_ready, 1)
            nc.gpsimd.iota(lane_i[:, :], pattern=[[0, 1]], base=0, channel_multiplier=1).then_inc(iota_ready, 1)

            def gather_tiles(slot, tiles, done):
                for j in tiles:
                    pool.indirect_dma_start(
                        rows[slot][:, j * D:(j + 1) * D], None, x,
                        bass.IndirectOffsetOnAxis(index[slot][:, j:j + 1], 0)).then_inc(done, 16)

            def gather(s):
                if not s.first:
                    pool.wait_ge(sums_ready, s.b - RING + 1)
                pool.wait_ge(index_loaded[s.slot], s.use * 16 + 16)
                pool.sem_inc(gathers_started, 1)
                gather_tiles(s.slot, range(POOLED), rows_gathered[s.slot])
                if s.first and s.slot == 0:
                    gather_tiles(s.slot, range(POOLED, TILES), first_gathered)

            batches(pool, gather)

            pool.wait_ge(span_ready, 1)
            reach = pool.value_load(span_max[0:1, 0:1], min_val=0, max_val=NODES)
            with pool.If(reach >= WINDOW):
                with pool.Fori(0, BATCHES) as b:
                    pool.wait_ge(far_loaded, b * 32 + 32)
                    pool.sem_inc(gathers_started, 1)
                    gather_tiles(0, range(TILES), far_gathered)

        @block.vector
        def _(dve):
            steps = [0]

            def own(ins):
                steps[0] += 1
                ins.then_inc(setup_step, 1)
                dve.wait_ge(setup_step, steps[0])

            nc.vector.memset(zeros[:, :], 0.0).then_inc(zeros_ready, 1)
            nc.vector.memset(x_stage[:, FULL, :], 0.0).then_inc(stage_cleared, 1)
            nc.vector.memset(feat[0][:, :].bitcast(F32), 0.0)
            nc.vector.memset(feat[1][:, :].bitcast(F32), 0.0)
            nc.vector.memset(lneps[:, :], LN_EPS)
            nc.vector.memset(one_one[:, :], 1.0)
            dve.wait_ge(src_loaded, 32)
            looked = src_b.rearrange("b (p j) -> b p j", j=TILES)[:, :, POOLED:TILES]

            def split(v):
                return v.rearrange("b (p j) -> b p j", j=LOOK)

            by_side, by_block = SIDE.bit_length() - 1, BLOCK.bit_length() - 1
            nc.vector.tensor_scalar(split(hi_i), looked, by_block, None, ALU.logical_shift_right)
            nc.vector.tensor_scalar(split(lo_i), looked, by_side, P - 1, ALU.logical_shift_right, ALU.bitwise_and)
            own(nc.vector.tensor_scalar(split(side_i), looked, SIDE - 1, None, ALU.bitwise_and))
            nc.vector.tensor_copy(feat_all[:, 0, :], hi_i)
            nc.vector.tensor_copy(feat_all[:, 1, :], lo_i)
            nc.vector.tensor_copy(feat_all[:, 2, :], side_i).then_inc(feat_ready, 1)
            dve.wait_ge(iota_ready, 3)
            nc.vector.tensor_scalar(side_of_i[:, :], lane_i[:, :], D.bit_length() - 1, None, ALU.logical_shift_right)
            nc.vector.tensor_copy(keys[:, :], keys_i[:, :])
            nc.vector.tensor_scalar(minus_keys[:, :], keys_i[:, :], -1.0, None, ALU.mult)
            own(nc.vector.tensor_copy(lane[:, :], lane_i[:, :]))
            nc.vector.tensor_copy(side_of[:, :], side_of_i[:, :])
            nc.vector.tensor_copy(iota[:, 0:WINDOW], iota_sb[:, :])
            nc.vector.tensor_scalar(ident[:, :], iota_sb[:, 0:P], lane[:, 0:1], None, ALU.is_equal).then_inc(ident_ready, 1)
            dve.wait_ge(ident_ready, 1)
            own(nc.vector.tensor_tensor(fold[:, :], ident[:, 0:D], ident[:, D:2 * D], ALU.add))
            for r in range(2, SIDE):
                own(nc.vector.tensor_tensor(fold[:, :], fold[:, :], ident[:, r * D:(r + 1) * D], ALU.add))
            own(nc.vector.scalar_tensor_tensor(key_rows[:, :], ident[:, 0:1], float(P), ident[:, 1:2], ALU.mult, ALU.add))
            nc.vector.tensor_copy(spread[:, 0, :], key_rows[:, :].to_broadcast([P, P]))
            nc.vector.tensor_copy(spread[:, 1, :], ident[:, 2:3].to_broadcast([P, P])).then_inc(spread_ready, 1)
            dve.wait_ge(dst_loaded, 16)
            nc.vector.tensor_reduce(dmin[:, :], dst_b, AX.X, ALU.min)
            own(nc.vector.tensor_reduce(dmax[:, :], dst_b, AX.X, ALU.max))
            nc.vector.tensor_copy(base_i[:, :], dmin[:, :])
            nc.vector.tensor_tensor(span[:, :], dmax[:, :], dmin[:, :], ALU.subtract).then_inc(bases_ready, 1)
            dve.wait_ge(stage_loaded, 32)
            for n in range(PARTS):
                done = nc.vector.tensor_copy(parts[:, :, n, :], x_stage[:, :, :])
                if n < PARTS - 1:
                    own(done)
                    own(nc.vector.tensor_tensor(x_stage[:, :, :], x_stage[:, :, :], parts[:, :, n, :], ALU.subtract))
                else:
                    done.then_inc(parts_ready, 1)
            dve.wait_ge(base_all_loaded, 32)
            own(nc.vector.tensor_tensor(rel[:, :, :], dst_sb,
                                        base_all[:, :].rearrange("p (b o) -> p b o", o=1).to_broadcast([P, BATCHES, TILES]),
                                        ALU.subtract))
            dve.wait_ge(base_rows_loaded, 32)
            nc.vector.tensor_reduce(span_max[0:1, 0:1], span_row[0:1, :], AX.X, ALU.max).then_inc(span_ready, 1)
            dve.wait_ge(small_loaded, 32)
            nc.vector.tensor_scalar(scale[:, :], scale[:, :], 1.0, None, ALU.add)
            nc.vector.tensor_scalar(ident_c[SUMS:P, :], ident[SUMS:P, SUMS:P], 1.0 / D, None, ALU.subtract)
            own(nc.vector.tensor_reduce(bias_mean[:, :], bias_row[:, 0, :], AX.X, ALU.add))
            own(nc.vector.tensor_scalar(bias_mean[:, :], bias_mean[:, :], 1.0 / D, None, ALU.mult))
            nc.vector.tensor_scalar(bias_row[:, :, :], bias_row[:, :, :], bias_mean[:, 0:1], None, ALU.subtract).then_inc(bias_ready, 1)
            dve.wait_ge(w_ready, 2)
            nc.vector.tensor_copy(bias_col[:, :], back_ps[:, D:D + 1])
            own(nc.vector.tensor_reduce(w_mean[:, :], back_ps[:, 0:D], AX.X, ALU.add))
            own(nc.vector.tensor_scalar(w_mean[:, :], w_mean[:, :], 1.0 / D, None, ALU.mult))
            own(nc.vector.tensor_scalar(wb[:, :], back_ps[:, 0:D], w_mean[:, 0:1], None, ALU.subtract))
            nc.vector.scalar_tensor_tensor(wb[SUMS:P, :], wb[SUMS:P, :], scale[SUMS:P, 0:1], ident_c[SUMS:P, :],
                                           ALU.mult, ALU.add).then_inc(wb_ready, 1)

            def mark(slot2, which, tiles):
                shape = [P, tiles.stop - tiles.start, WINDOW]
                return nc.vector.tensor_tensor(
                    onehot[slot2][:, tiles, :], iota[:, 0:WINDOW].rearrange("p (o w) -> p o w", o=1).to_broadcast(shape),
                    which.to_broadcast(shape), ALU.is_equal)

            def mark_batch(b, slot, part):
                slot2 = slot % 2
                if part == 0:
                    wait_count(dve, win_ready, b - 1)
                tiles = slice(part * MARK, (part + 1) * MARK)
                which = rel[:, bass.ds(b, 1), tiles].rearrange("p o j -> p (o j)").rearrange("p (j o) -> p j o", o=1)
                done = mark(slot2, which, tiles)
                if part == MARKS - 1:
                    done.then_inc(onehot_ready, 1)

            def add_window(b, slot):
                base = dve.value_load(base_row[0:1, bass.ds(b, 1)], min_val=0, max_val=NODES - 1)
                dve.wait_ge(win_ready, b + 1)
                if isinstance(b, int) and b == 0:
                    dve.wait_ge(aggX_cleared, 1)
                wait_count(dve, win_added, b)
                at = aggX[0:SUMS, bass.ds(base, WINDOW)]
                nc.vector.tensor_tensor(at, at, win[slot % 2][0:SUMS, 0:WINDOW], ALU.add).then_inc(win_added, 1)

            def add_rows(s):
                dve.wait_ge(rows_gathered[s.slot], s.use * (16 * POOLED) + 16 * POOLED)
                dve.wait_ge(edges_loaded[s.slot], s.use * 16 + 16)
                to, of = msg[s.slot], rows[s.slot]
                if s.first and s.slot == 0:
                    dve.wait_ge(first_gathered, 16 * LOOK)
                    nc.vector.tensor_tensor(to[:, :], of[:, :], to[:, :], ALU.add).then_inc(sums_ready, 1)
                else:
                    got, looked_up = slice(0, POOLED * D), slice(POOLED * D, ROW)
                    nc.vector.tensor_tensor(to[:, got], of[:, got], to[:, got], ALU.add).then_inc(sums_step, 1)
                    dve.wait_ge(back_ready, s.b)
                    dve.wait_ge(sums_step, s.b)
                    nc.vector.tensor_tensor(to[:, looked_up], back_ps[:, 0:LOOK * D], to[:, looked_up], ALU.add).then_inc(sums_ready, 1)

            def rest(to, high, done):
                to_v = to[:, :].rearrange("p (j f) -> p j f", f=D)
                nc.vector.scalar_tensor_tensor(to_v, to_v, 0.0, high, ALU.max, ALU.subtract).then_inc(done, 1)

            def rest_of(b, slot):
                dve.wait_ge(high_ready, b + 1)
                rest(msg[slot], msg_parts[slot % 2][:, :, 0, :], rest_ready)

            def low(to, mid, to_low, done):
                to_v = to[:, :].rearrange("p (j f) -> p j f", f=D)
                nc.vector.tensor_tensor(to_low, to_v, mid, ALU.subtract).then_inc(done, 1)

            def low_of(b, slot):
                dve.wait_ge(mid_ready, b + 1)
                low(msg[slot], msg_parts[slot % 2][:, :, 1, :], msg_parts[slot % 2][:, :, 2, :], msgs_ready)

            def look_up(k, slot2, i):
                bl = dve_blocks[i]
                dve.wait_ge(src_ready, k + 1)
                wait_count(dve, look_used, (k - 1) * BLOCKS + bl + 1)
                nc.vector.tensor_scalar(look[:, bl, :], src_ps[slot2][:, :], keys[:, bl:bl + 1], None,
                                        ALU.is_equal).then_inc(look_dve_ready, 1)

            def pick(s):
                dve.wait_ge(side_copied, s.b + 1)
                dve.wait_ge(look_used, s.b * BLOCKS + BLOCKS)
                wait_count(dve, back_ready, s.b)
                nc.vector.scalar_tensor_tensor(picked_sb[:, :], side_sb[:, :], side_of[:, 0:1], found_ps[:, :],
                                               ALU.is_equal, ALU.mult).then_inc(picked, 1)

            def batch(s):
                if s.first and s.slot == 0:
                    for i in range(AHEAD):
                        look_up(0, 0, i)
                if s.looks:
                    for i in range(AHEAD, BY_DVE):
                        look_up(s.b, s.slot % 2, i)
                        if reaches(s, 1):
                            if i in MARK_AT:
                                mark_batch(s.b - 1, s.slot - 1, MARK_AT.index(i))
                            if i == REST_AT:
                                rest_of(s.b - 1, (s.slot - 1) % RING)
                            if i == LOW_AT:
                                low_of(s.b - 1, (s.slot - 1) % RING)
                        if i == WINDOW_AT and reaches(s, 3):
                            add_window(s.b - 3, s.slot - 3)
                    if s.looks_on:
                        for i in range(AHEAD):
                            look_up(s.b + 1, (s.slot + 1) % 2, i)
                    pick(s)
                    add_rows(s)
                else:
                    for part in range(MARKS):
                        mark_batch(s.b - 1, s.slot - 1, part)
                    rest_of(s.b - 1, (s.slot - 1) % RING)
                    add_window(s.b - 3, s.slot - 3)
                    low_of(s.b - 1, (s.slot - 1) % RING)
                    for part in range(MARKS):
                        mark_batch(s.b, s.slot, part)
                    add_window(s.b - 2, s.slot - 2)
                    add_window(s.b - 1, s.slot - 1)
                    add_rows(s)
                    rest_of(s.b, s.slot)
                    low_of(s.b, s.slot)
                    add_window(s.b, s.slot)

            batches(dve, batch)

            dve.wait_ge(span_ready, 1)
            reach = dve.value_load(span_max[0:1, 0:1], min_val=0, max_val=NODES)
            dve.wait_ge(win_added, BATCHES)
            with dve.If(reach >= WINDOW):
                nc.vector.memset(far[:, :], 0.0).then_inc(far_added, 1)
                with dve.Fori(0, BATCHES) as b:
                    relb = rel[:, bass.ds(b, 1), :].rearrange("p o j -> p (o j)")
                    dve.wait_ge(far_gathered, b * (16 * TILES) + 16 * TILES)
                    dve.wait_ge(far_loaded, b * 32 + 32)
                    nc.vector.tensor_tensor(msg[0][:, :], rows[0][:, :], msg[0][:, :], ALU.add).then_inc(far_sums, 1)
                    dve.wait_ge(far_high, b + 1)
                    rest(msg[0], msg_parts[0][:, :, 0, :], far_rest)
                    dve.wait_ge(far_mid, b + 1)
                    low(msg[0], msg_parts[0][:, :, 1, :], msg_parts[0][:, :, 2, :], far_msgs)
                    nc.vector.tensor_scalar(far[:, :], relb, base_all[:, bass.ds(b, 1)], 1.0, ALU.add, ALU.add).then_inc(far_step, 1)
                    dve.wait_ge(far_step, b * (WINDOWS + 3) + 1)
                    nc.vector.scalar_tensor_tensor(far[:, :], relb, float(WINDOW), far[:, :], ALU.is_ge, ALU.mult).then_inc(far_step, 1)
                    dve.wait_ge(far_step, b * (WINDOWS + 3) + 2)
                    nc.vector.tensor_scalar(far[:, :], far[:, :], 1.0, None, ALU.subtract).then_inc(far_step, 1)
                    with dve.Fori(0, WINDOWS) as w:
                        dve.wait_ge(far_step, b * (WINDOWS + 3) + w + 3)
                        mark(0, far[:, :].rearrange("p (j o) -> p j o", o=1), slice(0, TILES)).then_inc(far_onehot, 1)
                        dve.wait_ge(far_onehot, b * WINDOWS + w + 1)
                        nc.vector.tensor_scalar(far[:, :], far[:, :], float(WINDOW), None, ALU.subtract).then_inc(far_step, 1)
                        dve.wait_ge(far_win, b * WINDOWS + w + 1)
                        at = aggX[0:SUMS, bass.ds(w * WINDOW, WINDOW)]
                        nc.vector.tensor_tensor(at, at, win[0][0:SUMS, 0:WINDOW], ALU.add).then_inc(far_added, 1)
                dve.wait_ge(far_added, BATCHES * WINDOWS + 1)
            nc.vector.memset(passes_done[:, :], 0.0).then_inc(agg_ready, 1)

            for k in range(len(ROUNDS_OUT) + 1):
                if k < len(ROUNDS_OUT):
                    t0, per = ROUNDS_OUT[k]
                    dve.wait_ge(sq_ready, k + 1)
                    nc.vector.tensor_reduce(var[:, t0:t0 + per * SIDE].rearrange("p (i r) -> p i r", i=per),
                                            z_round(sq_of(k), per), AX.X, ALU.add).then_inc(var_ready, 1)
                if k >= 1:
                    t0, per = ROUNDS_OUT[k - 1]
                    t = slice(t0, t0 + per * SIDE)
                    dve.wait_ge(std_ready, k)
                    nc.vector.reciprocal(rstd[:, t], rstd[:, t]).then_inc(rstd_ready, 1)
                    dve.wait_ge(rstd_ready, k)
                    nc.vector.tensor_tensor(
                        y_sb[:, t, :].rearrange("p (r i) f -> p i r f", i=per), z_round(z_of(k - 1), per),
                        rstd[:, t].rearrange("p (i r o) -> p i r o", i=per, o=1).to_broadcast([NP, per, SIDE, D]),
                        ALU.mult).then_inc(out_ready, 1)

        @block.scalar
        def _(act):
            act.dma_start(x_sb[:, :, :], x_v).then_inc(x_loaded, 16)
            act.dma_start(dst_b, dst_rows).then_inc(dst_loaded, 16)
            for r in range(P // D):
                act.dma_start(w_rep[:, r * D:(r + 1) * D], weight).then_inc(weights_loaded, 16)
            act.dma_start(scale[:, :], eps.rearrange("(a b) -> a b", a=1).to_broadcast([P, 1])).then_inc(small_loaded, 16)
            act.dma_start(bias_row[:, :, :], bias.rearrange("(a o f) -> a o f", a=1, o=1).to_broadcast([1, SIDE, D])).then_inc(small_loaded, 16)
            act.dma_start(dst_sb, dst_v).then_inc(base_all_loaded, 16)
            act.wait_ge(zeros_ready, 1)
            nc.scalar.copy(aggX[0:SUMS, :], zeros[0:SUMS, :].to_broadcast([SUMS, PAD])).then_inc(aggX_cleared, 1)

            for g in range(NT // TGROUP):
                act.wait_ge(xT_ready, g + 1)
                nc.scalar.copy(aggX_v[SUMS:P, g * TGROUP:(g + 1) * TGROUP, :], xT_group(g)).then_inc(x_copied, 1)

            def high_of(b, slot):
                act.wait_ge(sums_ready, b + 1)
                wait_count(act, win_ready, b - 1)
                nc.scalar.activation(msg_parts[slot % 2][:, :, 0, :], msg[slot][:, :].rearrange("p (j f) -> p j f", f=D),
                                     ACT.Relu).then_inc(high_ready, 1)

            def mid_of(b, slot):
                act.wait_ge(rest_ready, b + 1)
                nc.scalar.copy(msg_parts[slot % 2][:, :, 1, :], msg[slot][:, :].rearrange("p (j f) -> p j f", f=D)).then_inc(mid_ready, 1)

            def square(s, i):
                bl = act_blocks[i]
                wait_count(act, look_used, (s.b - 1) * BLOCKS + bl + 1)
                nc.scalar.activation(look[:, bl, :], key_sb[:, :], ACT.Square, bias=minus_keys[:, bl:bl + 1]).then_inc(squared, 1)

            def mark(s, i):
                bl = act_blocks[i]
                act.wait_ge(squared, s.b * BY_ACT + i + 1)
                nc.scalar.activation(look[:, bl, :], look[:, bl, :], ACT.Relu, scale=-2.0, bias=1.0).then_inc(look_act_ready, 1)

            def batch(s):
                if s.looks:
                    act.wait_ge(keys_ready, s.b + 1)
                    nc.scalar.copy(key_sb[:, :], act_ps[:, :]).then_inc(keys_copied, 1)
                    act.wait_ge(keys_copied, s.b + 1)
                    square(s, 0)
                    for i in range(BY_ACT):
                        if i + 1 < BY_ACT:
                            square(s, i + 1)
                        mark(s, i)
                        if i == HIGH_AT and reaches(s, 1):
                            high_of(s.b - 1, (s.slot - 1) % RING)
                        if i == MID_AT and reaches(s, 1):
                            mid_of(s.b - 1, (s.slot - 1) % RING)
                        if i == COPY_AT:
                            act.wait_ge(side_ready, s.b + 1)
                            wait_count(act, picked, s.b)
                            nc.scalar.copy(side_sb[:, :], act_ps[:, :]).then_inc(side_copied, 1)
                else:
                    high_of(s.b - 1, (s.slot - 1) % RING)
                    mid_of(s.b - 1, (s.slot - 1) % RING)
                    high_of(s.b, s.slot)
                    mid_of(s.b, s.slot)

            batches(act, batch)

            act.wait_ge(span_ready, 1)
            reach = act.value_load(span_max[0:1, 0:1], min_val=0, max_val=NODES)
            with act.If(reach >= WINDOW):
                with act.Fori(0, BATCHES) as b:
                    act.wait_ge(far_sums, b + 1)
                    to_v = msg[0][:, :].rearrange("p (j f) -> p j f", f=D)
                    nc.scalar.activation(msg_parts[0][:, :, 0, :], to_v, ACT.Relu).then_inc(far_high, 1)
                    act.wait_ge(far_rest, b + 1)
                    nc.scalar.copy(msg_parts[0][:, :, 1, :], to_v).then_inc(far_mid, 1)

            rounds = len(ROUNDS_OUT)
            for k in range(rounds + 2):
                if k < rounds:
                    cols = ROUNDS_OUT[k][1] * NP
                    act.wait_ge(zT_ready, k + 1)
                    if k >= 2:
                        act.wait_ge(z_ready, k - 1)
                    nc.scalar.activation(zT_sb[k % 2][:, 0:cols], zT[k % 2][:, 0:cols], ACT.Identity, bias=bias_col[:, 0:1]).then_inc(zT_copied, 1)
                if 1 <= k <= rounds:
                    act.wait_ge(z_ready, k)
                    if k >= 3:
                        act.wait_ge(var_ready, k - 2)
                    nc.scalar.activation(sq_of(k - 1), z_of(k - 1), ACT.Square).then_inc(sq_ready, 1)
                if k >= 2:
                    t0, per = ROUNDS_OUT[k - 2]
                    t = slice(t0, t0 + per * SIDE)
                    act.wait_ge(var_ready, k - 1)
                    nc.scalar.activation(rstd[:, t], var[:, t], ACT.Sqrt, bias=lneps[:, 0:1], scale=1.0 / D).then_inc(std_ready, 1)

        @block.tensor
        def _(pe):
            pe.wait_ge(ident_ready, 1)
            pe.wait_ge(weights_loaded, 16 * (P // D))
            nc.tensor.matmul(back_ps[:, 0:D], w_rep[:, :], ident[0:D, 0:D], start=True, stop=True).then_inc(w_ready, 1)
            pe.wait_ge(x_loaded, 16)
            for g in range(NT // TGROUP):
                if g >= 2:
                    pe.wait_ge(x_copied, g - 1)
                for t in range(TGROUP):
                    last = nc.tensor.transpose(xT[g % 2][0:D, t * NP:(t + 1) * NP], x_sb[:, g * TGROUP + t, :],
                                               ident[0:NP, 0:NP])
                last.then_inc(xT_ready, 1)

            pe.wait_ge(bias_ready, 1)
            nc.tensor.matmul(back_ps[:, D:D + 1], bias_row[:, :, :].rearrange("o r f -> o (r f)"), one_one[:, :], start=True, stop=True).then_inc(w_ready, 1)

            def sum_tiles(slot2, tiles):
                for j in tiles:
                    last = nc.tensor.matmul(win[slot2][0:SUMS, 0:WINDOW], msg_parts[slot2][:, j, :, :].rearrange("p n f -> p (n f)"),
                                            onehot[slot2][:, j, :], start=(j == 0), stop=(j == TILES - 1))
                return last

            def sum_batch(b, slot, part):
                if part == 0:
                    wait_count(pe, win_added, b - 1)
                    pe.wait_ge(onehot_ready, b + 1)
                    pe.wait_ge(msgs_ready, b + 1)
                last = sum_tiles(slot % 2, range(part * MARK, (part + 1) * MARK))
                if part == MARKS - 1:
                    last.then_inc(win_ready, 1)

            def turn_back(s):
                pe.wait_ge(picked, s.b)
                pe.wait_ge(sums_ready, s.b)
                picked_v = picked_sb[:, :].rearrange("r (p j) -> r j p", j=LOOK)
                for j in range(LOOK):
                    last = nc.tensor.matmul(back_ps[:, j * D:(j + 1) * D], picked_v[:, j, :], fold[:, :], start=True, stop=True)
                last.then_inc(back_ready, 1)

            def spread_keys(k, slot2, turns):
                pe.wait_ge(feat_loaded[slot2], turns * 16 + 16)
                nc.tensor.matmul(src_ps[slot2][:, :], spread[:, 0, :], feat[slot2][:, :], start=True, stop=True).then_inc(src_ready, 1)
                wait_count(pe, side_copied, k)
                nc.tensor.matmul(act_ps[:, :], spread[:, 0, :], feat[slot2][:, :], start=True, stop=True).then_inc(keys_ready, 1)

            def look_up(s):
                a = d = 0
                for bl in range(BLOCKS):
                    if bl % SUM_EVERY == 0 and reaches(s, 2):
                        sum_batch(s.b - 2, (s.slot - 2) % RING, bl // SUM_EVERY)
                    if bl == BACK_AT and reaches(s, 1):
                        turn_back(s)
                    if bl == SIDE_AT:
                        pe.wait_ge(keys_copied, s.b + 1)
                        nc.tensor.matmul(act_ps[:, :], spread[:, 1, :], feat[s.slot % 2][:, :], start=True, stop=True).then_inc(side_ready, 1)
                    if bl == SRC_AT and s.looks_on:
                        spread_keys(s.b + 1, (s.slot + 1) % 2, s.turns + s.slot % 2)
                    if bl == 0:
                        wait_count(pe, picked, s.b)
                    if by_act[bl]:
                        a += 1
                        pe.wait_ge(look_act_ready, s.b * BY_ACT + a)
                    else:
                        d += 1
                        pe.wait_ge(look_dve_ready, s.b * BY_DVE + d)
                    for n in range(PARTS):
                        last = nc.tensor.matmul(found_ps[:, :], parts[:, bl, n, :], look[:, bl, :],
                                                start=(bl == 0 and n == 0), stop=(bl == BLOCKS - 1 and n == PARTS - 1))
                    last.then_inc(look_used, 1)

            def batch(s):
                if s.first and s.slot == 0:
                    pe.wait_ge(spread_ready, 1)
                    spread_keys(0, 0, 0)
                    pe.wait_ge(parts_ready, 1)
                    pe.wait_ge(wb_ready, 1)
                    pe.wait_ge(x_copied, NT // TGROUP)
                if s.looks:
                    look_up(s)
                else:
                    turn_back(s)
                    for b in range(BATCHES - 3, BATCHES):
                        for part in range(MARKS):
                            sum_batch(b, b % RING, part)

            batches(pe, batch)

            pe.wait_ge(span_ready, 1)
            reach = pe.value_load(span_max[0:1, 0:1], min_val=0, max_val=NODES)
            with pe.If(reach >= WINDOW):
                with pe.Fori(0, BATCHES) as b:
                    with pe.Fori(0, WINDOWS) as w:
                        pe.wait_ge(far_msgs, b + 1)
                        pe.wait_ge(far_added, b * WINDOWS + w + 1)
                        pe.wait_ge(far_onehot, b * WINDOWS + w + 1)
                        sum_tiles(0, range(TILES)).then_inc(far_win, 1)

            pe.wait_ge(agg_ready, 1)
            for k in range(len(ROUNDS_OUT) + 1):
                if k < len(ROUNDS_OUT):
                    t0, per = ROUNDS_OUT[k]
                    if k >= 2:
                        pe.wait_ge(zT_copied, k - 1)
                    for r in range(SIDE):
                        last = nc.tensor.matmul(zT[k % 2][r * D:(r + 1) * D, 0:per * NP], wb[:, :],
                                                aggX_v[:, t0 + r * per:t0 + (r + 1) * per, :], start=True, stop=True)
                    last.then_inc(zT_ready, 1)
                if k >= 1:
                    per = ROUNDS_OUT[k - 1][1]
                    pe.wait_ge(zT_copied, k)
                    if k >= 3:
                        pe.wait_ge(out_ready, k - 2)
                    for i in range(per):
                        last = nc.tensor.transpose(z[(k - 1) % 2][0:NP, i * P:(i + 1) * P], zT_sb[(k - 1) % 2][:, i * NP:(i + 1) * NP], ident[:, :])
                    last.then_inc(z_ready, 1)


def kernel(x, src, dst, edge_attr_32, L0_gnn_W, L0_gnn_b, L0_gnn_eps):
    import numpy as np
    import concourse.bacc as bacc
    from concourse import mybir as mb
    from concourse.bass_utils import run_bass_kernel_spmd

    given = {"x": x, "src": src, "dst": dst, "edge": edge_attr_32, "weight": L0_gnn_W, "bias": L0_gnn_b, "eps": L0_gnn_eps}
    arrays = {f"in_{n}": np.ascontiguousarray(a) for n, a in given.items()}
    nc = bacc.Bacc("TRN2", target_bir_lowering=False, num_devices=1)
    args = [nc.dram_tensor(n, a.shape, mb.dt.from_np(a.dtype), kind="ExternalInput").ap() for n, a in arrays.items()]
    out = nc.dram_tensor("out", list(x.shape), mb.dt.float32, kind="ExternalOutput").ap()
    gnn_kernel(nc, *args, out)
    r = run_bass_kernel_spmd(nc, [arrays], core_ids=[0])
    return r.results[0]["out"]
```

```python
import concourse.bass as bass
from concourse import mybir
from collections import namedtuple
from contextlib import ExitStack

Step = namedtuple("Step", "b slot use first last looks looks_on turns")

P = 128
PARTS = 3
FEATURES = 3


def gnn_kernel(nc, x, src, dst, edge, weight, bias, eps, out):
    F32, I32, BF16 = mybir.dt.float32, mybir.dt.int32, mybir.dt.bfloat16
    ALU, ACT, AX = mybir.AluOpType, mybir.ActivationFunctionType, mybir.AxisListType

    NODES, D = x.shape
    EDGES = src.shape[0]
    TILES = 23
    SHORT = EDGES // P % TILES
    BATCH, FIRST = P * TILES, P * SHORT
    BATCHES = (EDGES - FIRST) // BATCH + 1
    HALF = BATCHES // 2
    RING = 4
    PEEL = RING + 1
    LAST = (BATCHES - PEEL) % RING + RING
    ROUNDS = (BATCHES - PEEL - LAST) // RING
    ROW = TILES * D
    LOOK = 4
    POOLED = TILES - LOOK
    COLS = P * LOOK
    SIDE = P // D
    BLOCK = P * SIDE
    BLOCKS = -(-NODES // BLOCK)
    FULL = NODES // BLOCK
    REST = (NODES - FULL * BLOCK) // SIDE
    BY_ACT = 12
    BY_DVE = BLOCKS - BY_ACT
    AHEAD = 3
    WINDOW = 128
    WINDOWS = -(-NODES // WINDOW)
    PAD = (WINDOWS + 1) * WINDOW
    SUMS = PARTS * D
    MARK = 5
    MARKS = -(-TILES // MARK)
    SUM_EVERY, SIDE_AT, BACK_AT, SRC_AT = BLOCKS // MARKS, 6, 10, 20
    HIGH_AT, MID_AT, COPY_AT = 2, 7, 5
    CLEARS = 4
    MARK_AT, REST_AT, WINDOW_AT, LOW_AT = (3, 4, 6, 8, 9), 5, 7, 11
    NP = 125
    NT = NODES // NP
    TGROUP = 4
    OGROUP = 4
    ROUNDS_OUT = [(0, NT // SIDE % OGROUP)] + [(t, OGROUP) for t in range(NT % (OGROUP * SIDE), NT, OGROUP * SIDE)]
    LN_EPS = 1e-5
    ZRING = 4
    assert EDGES == FIRST + BATCH * (BATCHES - 1) and POOLED <= SHORT and BATCHES == 2 * HALF and HALF <= P
    assert PAD % CLEARS == 0 and 3 * CLEARS <= BY_ACT
    assert NODES == NP * NT and NT % TGROUP == 0 and NT % SIDE == 0 and NT // SIDE % OGROUP > 0 and SUMS + D == P
    assert BLOCKS % MARKS == 0 and NODES % SIDE == 0

    by_act = [(i + 1) * BY_ACT // BLOCKS > i * BY_ACT // BLOCKS for i in range(BLOCKS)]
    act_blocks = [i for i in range(BLOCKS) if by_act[i]]
    dve_blocks = [i for i in range(BLOCKS) if not by_act[i]]

    src_v = src[FIRST:].rearrange("(b p j) -> b p j", p=P, j=TILES)
    src_rows = src[FIRST:].rearrange("(b e) -> b e", e=BATCH)
    dst_v = dst[FIRST:].rearrange("(b p j) -> p b j", p=P, j=TILES)
    dst_rows = dst[FIRST:].rearrange("(b e) -> b e", e=BATCH)
    edge_v = edge[FIRST:, :].rearrange("(b p j) f -> b p (j f)", p=P, j=TILES)
    src_first = src[0:FIRST].rearrange("(p j) -> p j", j=SHORT)
    dst_first = dst[0:FIRST].rearrange("(p j) -> p j", j=SHORT)
    edge_first = edge[0:FIRST, :].rearrange("(p j) f -> p (j f)", j=SHORT)
    x_v = x.rearrange("(p t) f -> p t f", t=NT)
    x_blocks = x[0:FULL * BLOCK, :].rearrange("(b p s) f -> p b (s f)", p=P, s=SIDE)
    x_rest = x[FULL * BLOCK:, :].rearrange("(p s) f -> p (s f)", s=SIDE)
    out_v = out.rearrange("(p t) f -> p t f", t=NT)
    base_dram = nc.dram_tensor("base_dram", [1, BATCHES], F32, kind="Internal").ap()
    feat_dram = nc.dram_tensor("feat_dram", [BATCHES, FEATURES, COLS], BF16, kind="Internal").ap()

    ctx = ExitStack()
    with ctx:
        def sb(name, shape, dt=F32):
            return ctx.enter_context(nc.sbuf_tensor(name, shape, dt))

        def ps(name):
            return ctx.enter_context(nc.psum_tensor(name, [P, 512], F32))

        def sem(name):
            return ctx.enter_context(nc.semaphore(name))

        index = [sb(f"index{s}", [P, TILES], I32) for s in range(RING)]
        rows = [sb(f"rows{s}", [P, ROW]) for s in range(RING)]
        msg = [sb(f"msg{s}", [P, ROW]) for s in range(RING)]
        msg_parts = [sb(f"msg_parts{s}", [P, TILES, PARTS, D], BF16) for s in range(2)]
        onehots = sb("onehots", [P, 2, TILES, WINDOW], BF16)
        onehot = [onehots[:, s, :, :] for s in range(2)]
        win = [ps(f"win{s}") for s in range(2)]
        parts = sb("parts", [P, BLOCKS, PARTS, P], BF16)
        keys = sb("keys", [P, BLOCKS])
        minus_keys = sb("minus_keys", [P, BLOCKS])
        feat = [sb(f"feat{s}", [P, COLS], BF16) for s in range(2)]
        spread = sb("spread", [P, 2, P], BF16)
        look = sb("look", [P, BLOCKS, COLS], BF16)
        side_of = sb("side_of", [P, 1])
        side_sb = sb("side_sb", [P, COLS])
        picked_sb = sb("picked_sb", [P, COLS])
        fold = sb("fold", [P, D])
        src_ps = ps("src_ps")
        key_sb = sb("key_sb", [P, COLS])
        side_ps = ps("side_ps")
        found_ps = [ps(f"found_ps{s}") for s in range(2)]
        back_ps = ps("back_ps")
        aggX = sb("aggX", [P, PAD])
        x_sb = sb("x_sb", [NP, NT, D])
        rel = sb("rel", [P, BATCHES, TILES])
        dst_sb = rel[:, :, :].bitcast(I32)
        base_all = sb("base_all", [P, BATCHES])
        base_row = sb("base_row", [1, BATCHES], I32)
        span_row = sb("span_row", [1, BATCHES])
        span_max = sb("span_max", [1, 1], I32)
        wb = sb("wb", [P, D])
        bias_row = sb("bias_row", [1, SIDE, D])
        bias_col = sb("bias_col", [P, 1])
        one_one = sb("one_one", [1, 1])
        x_stage = sb("x_stage", [P, BLOCKS, P])
        zeros = sb("zeros", [P, 1])
        dst_b = aggX[0:HALF, 0:2 * BATCH].rearrange("p (s e) -> p s e", s=2).bitcast(I32)
        src_b = look[0:HALF, :, :].rearrange("p b c -> p (b c)").bitcast(I32)[:, 0:2 * BATCH].rearrange("p (s e) -> p s e", s=2)
        hi_i, lo_i, side_i = (
            aggX[0:HALF, at:at + 2 * COLS].rearrange("p (s c) -> p s c", s=2).bitcast(I32)
            for at in range(2 * BATCH, 2 * BATCH + 3 * 2 * COLS, 2 * COLS))
        dmin = sb("dmin", [HALF, 2])
        dmax = sb("dmax", [HALF, 2])
        base_i = sb("base_i", [HALF, 2], I32)
        span = sb("span", [HALF, 2])
        feat_all = sb("feat_all", [HALF, 2, FEATURES, COLS], BF16)
        keys_i = sb("keys_i", [P, BLOCKS], I32)
        side_of_i = sb("side_of_i", [P, 1], I32)
        key_rows = sb("key_rows", [P, 1])
        iota_sb = sb("iota_sb", [P, WINDOW], I32)
        lane_i = sb("lane_i", [P, 1], I32)
        lane = sb("lane", [P, 1])
        ident = sb("ident", [P, P])
        scale = sb("scale", [P, 1])
        w_rep = sb("w_rep", [D, P])
        w_mean = sb("w_mean", [P, 1])
        ident_c = sb("ident_c", [P, D])
        bias_mean = sb("bias_mean", [1, 1])
        far = sb("far", [P, TILES])
        passes_done = sb("passes_done", [1, 1])
        lneps = sb("lneps", [NP, 1])
        iota = ps("iota")
        xT = win
        zT = win + [src_ps, iota]
        z = found_ps + [back_ps, side_ps]
        y_sb = x_sb
        var = sb("var", [NP, NT])
        rstd = sb("rstd", [NP, NT])
        zT_sb = rows
        sq = msg

        index_loaded = [sem(f"index_loaded{s}") for s in range(RING)]
        edges_loaded = [sem(f"edges_loaded{s}") for s in range(RING)]
        rows_gathered = [sem(f"rows_gathered{s}") for s in range(RING)]
        first_gathered = sem("first_gathered")
        gathers_started = sem("gathers_started")
        sums_ready = sem("sums_ready")
        sums_step = sem("sums_step")
        high_ready = sem("high_ready")
        rest_ready = sem("rest_ready")
        mid_ready = sem("mid_ready")
        msgs_ready = sem("msgs_ready")
        onehot_ready = sem("onehot_ready")
        win_ready = sem("win_ready")
        win_added = sem("win_added")
        feat_loaded = [sem(f"feat_loaded{s}") for s in range(2)]
        src_ready = sem("src_ready")
        keys_copied = sem("keys_copied")
        side_ready = sem("side_ready")
        squared = sem("squared")
        look_act_ready = sem("look_act_ready")
        look_dve_ready = sem("look_dve_ready")
        look_used = sem("look_used")
        side_copied = sem("side_copied")
        picked = sem("picked")
        back_ready = sem("back_ready")
        dst_loaded = sem("dst_loaded")
        src_loaded = sem("src_loaded")
        x_loaded = sem("x_loaded")
        zeros_ready = sem("zeros_ready")
        aggX_cleared = sem("aggX_cleared")
        stage_cleared = sem("stage_cleared")
        bias_ready = sem("bias_ready")
        stage_loaded = sem("stage_loaded")
        weights_loaded = sem("weights_loaded")
        small_loaded = sem("small_loaded")
        spread_ready = sem("spread_ready")
        parts_ready = sem("parts_ready")
        feat_ready = sem("feat_ready")
        feat_written = sem("feat_written")
        bases_ready = sem("bases_ready")
        base_written = sem("base_written")
        base_rows_loaded = sem("base_rows_loaded")
        base_all_loaded = sem("base_all_loaded")
        iota_ready = sem("iota_ready")
        ident_ready = sem("ident_ready")
        setup_step = sem("setup_step")
        w_ready = sem("w_ready")
        wb_ready = sem("wb_ready")
        xT_ready = sem("xT_ready")
        x_copied = sem("x_copied")
        span_ready = sem("span_ready")
        agg_ready = sem("agg_ready")
        zT_ready = sem("zT_ready")
        zT_copied = sem("zT_copied")
        z_ready = sem("z_ready")
        sq_ready = sem("sq_ready")
        var_ready = sem("var_ready")
        std_ready = sem("std_ready")
        rstd_ready = sem("rstd_ready")
        out_ready = sem("out_ready")
        out_stored = sem("out_stored")
        far_loaded = sem("far_loaded")
        far_gathered = sem("far_gathered")
        far_sums = sem("far_sums")
        far_high = sem("far_high")
        far_rest = sem("far_rest")
        far_mid = sem("far_mid")
        far_msgs = sem("far_msgs")
        far_step = sem("far_step")
        far_onehot = sem("far_onehot")
        far_win = sem("far_win")
        far_added = sem("far_added")

        block = ctx.enter_context(nc.Block())

        def batches(eng, step):
            def at(b, rounds):
                step(Step(b=rounds * RING + b, slot=b % RING, use=rounds + b // RING, first=b < RING, last=b == BATCHES - 1,
                          looks=b < BATCHES - 1, looks_on=b < BATCHES - 2, turns=rounds * (RING // 2) + b // 2))

            for b in range(PEEL):
                at(b, 0)
            with eng.Fori(0, ROUNDS) as i:
                for u in range(RING):
                    at(PEEL + u, i)
            for b in range(BATCHES - LAST, BATCHES):
                at(b, 0)

        def reaches(s, n):
            return not s.first or s.slot >= n

        def tiles_of(b):
            return SHORT if isinstance(b, int) and b == 0 else TILES

        def row_of(b):
            return (b - 1) % BATCHES if isinstance(b, int) else b - 1

        def messages(s, n):
            return msg[s][:, 0:n * D].rearrange("p (j f) -> p j f", f=D)

        def parts_of(s, n, part):
            return msg_parts[s % 2][:, 0:n, part, :]

        def wait_count(eng, semaphore, count):
            if not (isinstance(count, int) and count <= 0):
                eng.wait_ge(semaphore, count)

        aggX_v = aggX[:, 0:NODES].rearrange("f (p t) -> f t p", t=NT)

        def xT_group(g):
            return xT[g % 2][0:D, 0:TGROUP * NP].rearrange("f (t p) -> f t p", p=NP)

        def z_round(v, per):
            return v.rearrange("p (i r f) -> p i r f", i=per, f=D)

        def z_of(k):
            return z[k % ZRING][0:NP, 0:ROUNDS_OUT[k][1] * P]

        def sq_of(k):
            return sq[k % ZRING][0:NP, 0:ROUNDS_OUT[k][1] * P]

        def one(ap3, b):
            return ap3[bass.ds(b, 1), :, :].rearrange("o p f -> (o p) f")

        def feat_of(k):
            return feat_dram[bass.ds(k, 1), :, :].rearrange("o r c -> (o r) c")

        ROW_LOADS = 5

        def load_rows(eng, to, values, in_rows, done):
            k = HALF // 16 * 16
            for s in range(2):
                eng.dma_start(to[0:k, s, :], in_rows[s * HALF:s * HALF + k, :]).then_inc(done, 16)
            eng.dma_start(to[k:HALF, 0, :], in_rows[k:HALF, :]).then_inc(done, 16)
            eng.dma_start(to[k:HALF - 1, 1, :], in_rows[HALF + k:BATCHES - 1, :]).then_inc(done, 16)
            eng.dma_start(to[HALF - 1:HALF, 1, :], values[0:BATCH].rearrange("(o e) -> o e", o=1)).then_inc(done, 16)

        @block.sync
        def _(sp):
            sp.dma_start(index[0][:, 0:SHORT], src_first).then_inc(index_loaded[0], 16)
            for b in range(1, RING):
                sp.dma_start(index[b][:, :], src_v[b - 1]).then_inc(index_loaded[b], 16)
            load_rows(sp, src_b, src, src_rows, src_loaded)
            sp.wait_ge(stage_cleared, 1)
            sp.dma_start(x_stage[:, 0:FULL, :], x_blocks).then_inc(stage_loaded, 16)
            sp.dma_start(x_stage[0:REST, FULL, :], x_rest).then_inc(stage_loaded, 16)
            sp.wait_ge(feat_ready, 1)
            sp.dma_start(feat_dram.rearrange("(s p) r c -> p s r c", s=2), feat_all[:, :, :, :]).then_inc(feat_written, 16)
            sp.wait_ge(feat_written, 16)
            sp.dma_start(feat[0][0:FEATURES, :], feat_of(0)).then_inc(feat_loaded[0], 16)

            def load(s):
                if not s.first:
                    sp.wait_ge(rows_gathered[s.slot], s.use * (16 * POOLED))
                    sp.dma_start(index[s.slot][:, :], one(src_v, s.b - 1)).then_inc(index_loaded[s.slot], 16)
                    sp.wait_ge(msgs_ready, s.b - RING + 1)
                if s.first and s.slot == 0:
                    sp.dma_start(msg[0][:, 0:SHORT * D], edge_first).then_inc(edges_loaded[0], 16)
                else:
                    sp.dma_start(msg[s.slot][:, :], one(edge_v, s.b - 1)).then_inc(edges_loaded[s.slot], 16)
                if s.looks and not (s.first and s.slot == 0):
                    wait_count(sp, side_ready, s.b - 1)
                    sp.dma_start(feat[s.slot % 2][0:FEATURES, :], feat_of(s.b)).then_inc(feat_loaded[s.slot % 2], 16)

            def spread_bases():
                sp.wait_ge(bases_ready, 1)
                for s in range(2):
                    sp.dma_start(base_dram[:, s * HALF:(s + 1) * HALF].rearrange("o b -> b o"), dmin[:, s:s + 1]).then_inc(base_written, 16)
                    sp.dma_start(base_row[0:1, s * HALF:(s + 1) * HALF], base_i[:, s:s + 1]).then_inc(base_rows_loaded, 16)
                    sp.dma_start(span_row[0:1, s * HALF:(s + 1) * HALF], span[:, s:s + 1]).then_inc(base_rows_loaded, 16)
                sp.wait_ge(base_written, 32)
                sp.dma_start(base_all[:, :], base_dram.to_broadcast([P, BATCHES])).then_inc(base_all_loaded, 16)

            def step(s):
                load(s)
                if s.first and s.slot == 1:
                    spread_bases()

            batches(sp, step)

            sp.wait_ge(span_ready, 1)
            reach = sp.value_load(span_max[0:1, 0:1], min_val=0, max_val=NODES)
            with sp.If(reach >= WINDOW):
                sp.wait_ge(far_added, 1)
                sp.dma_start(index[0][:, 0:SHORT], src_first).then_inc(far_loaded, 16)
                sp.dma_start(msg[0][:, 0:SHORT * D], edge_first).then_inc(far_loaded, 16)
                with sp.Fori(0, BATCHES - 1) as row:
                    sp.wait_ge(far_added, row * WINDOWS + (WINDOWS + 1))
                    sp.dma_start(index[0][:, :], one(src_v, row)).then_inc(far_loaded, 16)
                    sp.dma_start(msg[0][:, :], one(edge_v, row)).then_inc(far_loaded, 16)

            for k, (t0, per) in enumerate(ROUNDS_OUT):
                t = slice(t0, t0 + per * SIDE)
                sp.wait_ge(out_ready, k + 1)
                sp.dma_start(out_v[:, t, :], y_sb[:, t, :]).then_inc(out_stored, 16)
            sp.wait_ge(out_stored, 16 * len(ROUNDS_OUT))

        @block.gpsimd
        def _(pool):
            nc.gpsimd.iota(iota_sb[:, :], pattern=[[1, WINDOW]], base=0, channel_multiplier=0).then_inc(iota_ready, 1)
            nc.gpsimd.iota(keys_i[:, :], pattern=[[P, BLOCKS]], base=0, channel_multiplier=1).then_inc(iota_ready, 1)
            nc.gpsimd.iota(lane_i[:, :], pattern=[[0, 1]], base=0, channel_multiplier=1).then_inc(iota_ready, 1)

            def gather_tiles(slot, tiles, done):
                for j in tiles:
                    pool.indirect_dma_start(
                        rows[slot][:, j * D:(j + 1) * D], None, x,
                        bass.IndirectOffsetOnAxis(index[slot][:, j:j + 1], 0)).then_inc(done, 16)

            def gather(s):
                if not s.first:
                    pool.wait_ge(sums_ready, s.b - RING + 1)
                pool.wait_ge(index_loaded[s.slot], s.use * 16 + 16)
                pool.sem_inc(gathers_started, 1)
                if s.first and s.slot == 0:
                    gather_tiles(s.slot, range(POOLED, SHORT), first_gathered)
                gather_tiles(s.slot, range(POOLED), rows_gathered[s.slot])

            batches(pool, gather)

            pool.wait_ge(span_ready, 1)
            reach = pool.value_load(span_max[0:1, 0:1], min_val=0, max_val=NODES)
            with pool.If(reach >= WINDOW):
                pool.wait_ge(far_loaded, 32)
                gather_tiles(0, range(SHORT), far_gathered)
                with pool.Fori(0, BATCHES - 1) as row:
                    pool.wait_ge(far_loaded, row * 32 + 64)
                    pool.sem_inc(gathers_started, 1)
                    gather_tiles(0, range(TILES), far_gathered)

        @block.vector
        def _(dve):
            steps = [0]

            def own(ins):
                steps[0] += 1
                ins.then_inc(setup_step, 1)
                dve.wait_ge(setup_step, steps[0])

            nc.vector.memset(zeros[:, :], 0.0).then_inc(zeros_ready, 1)
            nc.vector.memset(x_stage[:, FULL, :], 0.0).then_inc(stage_cleared, 1)
            nc.vector.memset(feat[0][:, :].bitcast(F32), 0.0)
            nc.vector.memset(feat[1][:, :].bitcast(F32), 0.0)
            nc.vector.memset(lneps[:, :], LN_EPS)
            nc.vector.memset(one_one[:, :], 1.0)
            dve.wait_ge(src_loaded, 16 * ROW_LOADS)
            looked = src_b.rearrange("b s (p j) -> b s p j", j=TILES)[:, :, :, POOLED:TILES]

            def split(v):
                return v.rearrange("b s (p j) -> b s p j", j=LOOK)

            by_side, by_block = SIDE.bit_length() - 1, BLOCK.bit_length() - 1
            nc.vector.tensor_scalar(split(hi_i), looked, by_block, None, ALU.logical_shift_right)
            nc.vector.tensor_scalar(split(lo_i), looked, by_side, P - 1, ALU.logical_shift_right, ALU.bitwise_and)
            own(nc.vector.tensor_scalar(split(side_i), looked, SIDE - 1, None, ALU.bitwise_and))
            nc.vector.tensor_copy(feat_all[:, :, 0, :], hi_i)
            nc.vector.tensor_copy(feat_all[:, :, 1, :], lo_i)
            nc.vector.tensor_copy(feat_all[:, :, 2, :], side_i).then_inc(feat_ready, 1)
            dve.wait_ge(iota_ready, 3)
            nc.vector.tensor_scalar(side_of_i[:, :], lane_i[:, :], D.bit_length() - 1, None, ALU.logical_shift_right)
            nc.vector.tensor_copy(keys[:, :], keys_i[:, :])
            nc.vector.tensor_scalar(minus_keys[:, :], keys_i[:, :], -1.0, None, ALU.mult)
            own(nc.vector.tensor_copy(lane[:, :], lane_i[:, :]))
            nc.vector.tensor_copy(side_of[:, :], side_of_i[:, :])
            nc.vector.tensor_copy(iota[:, 0:WINDOW], iota_sb[:, :])
            nc.vector.tensor_scalar(ident[:, :], iota_sb[:, 0:P], lane[:, 0:1], None, ALU.is_equal).then_inc(ident_ready, 1)
            dve.wait_ge(ident_ready, 1)
            own(nc.vector.tensor_tensor(fold[:, :], ident[:, 0:D], ident[:, D:2 * D], ALU.add))
            for r in range(2, SIDE):
                own(nc.vector.tensor_tensor(fold[:, :], fold[:, :], ident[:, r * D:(r + 1) * D], ALU.add))
            own(nc.vector.scalar_tensor_tensor(key_rows[:, :], ident[:, 0:1], float(P), ident[:, 1:2], ALU.mult, ALU.add))
            nc.vector.tensor_copy(spread[:, 0, :], key_rows[:, :].to_broadcast([P, P]))
            nc.vector.tensor_copy(spread[:, 1, :], ident[:, 2:3].to_broadcast([P, P])).then_inc(spread_ready, 1)
            dve.wait_ge(small_loaded, 32)
            nc.vector.tensor_scalar(scale[:, :], scale[:, :], 1.0, None, ALU.add)
            nc.vector.tensor_scalar(ident_c[SUMS:P, :], ident[SUMS:P, SUMS:P], 1.0 / D, None, ALU.subtract)
            own(nc.vector.tensor_reduce(bias_mean[:, :], bias_row[:, 0, :], AX.X, ALU.add))
            own(nc.vector.tensor_scalar(bias_mean[:, :], bias_mean[:, :], 1.0 / D, None, ALU.mult))
            nc.vector.tensor_scalar(bias_row[:, :, :], bias_row[:, :, :], bias_mean[:, 0:1], None, ALU.subtract).then_inc(bias_ready, 1)
            dve.wait_ge(w_ready, 2)
            nc.vector.tensor_copy(bias_col[:, :], back_ps[:, D:D + 1])
            own(nc.vector.tensor_reduce(w_mean[:, :], back_ps[:, 0:D], AX.X, ALU.add))
            own(nc.vector.tensor_scalar(w_mean[:, :], w_mean[:, :], 1.0 / D, None, ALU.mult))
            own(nc.vector.tensor_scalar(wb[:, :], back_ps[:, 0:D], w_mean[:, 0:1], None, ALU.subtract))
            nc.vector.scalar_tensor_tensor(wb[SUMS:P, :], wb[SUMS:P, :], scale[SUMS:P, 0:1], ident_c[SUMS:P, :],
                                           ALU.mult, ALU.add).then_inc(wb_ready, 1)

            dve.wait_ge(stage_loaded, 32)
            for n in range(PARTS):
                done = nc.vector.tensor_copy(parts[:, :, n, :], x_stage[:, :, :])
                if n < PARTS - 1:
                    own(done)
                    own(nc.vector.tensor_tensor(x_stage[:, :, :], x_stage[:, :, :], parts[:, :, n, :], ALU.subtract))
                else:
                    done.then_inc(parts_ready, 1)
            def find_bases():
                dve.wait_ge(dst_loaded, 16 * ROW_LOADS)
                nc.vector.tensor_reduce(dmin[:, :], dst_b, AX.X, ALU.min)
                own(nc.vector.tensor_reduce(dmax[:, :], dst_b, AX.X, ALU.max))
                nc.vector.tensor_copy(base_i[:, :], dmin[:, :])
                nc.vector.tensor_tensor(span[:, :], dmax[:, :], dmin[:, :], ALU.subtract).then_inc(bases_ready, 1)

            def place_edges():
                dve.wait_ge(base_all_loaded, 48)
                bases = base_all[:, :].rearrange("p (b o) -> p b o", o=1)
                for some, n in (slice(0, BATCHES - 1), TILES), (slice(BATCHES - 1, BATCHES), SHORT):
                    own(nc.vector.tensor_tensor(rel[:, some, 0:n], dst_sb[:, some, 0:n],
                                                bases[:, some, :].to_broadcast([P, some.stop - some.start, n]), ALU.subtract))
                dve.wait_ge(base_rows_loaded, 64)
                nc.vector.tensor_reduce(span_max[0:1, 0:1], span_row[0:1, :], AX.X, ALU.max).then_inc(span_ready, 1)

            def mark(slot2, which, tiles):
                shape = [P, tiles.stop - tiles.start, WINDOW]
                return nc.vector.tensor_tensor(
                    onehot[slot2][:, tiles, :], iota[:, 0:WINDOW].rearrange("p (o w) -> p o w", o=1).to_broadcast(shape),
                    which.to_broadcast(shape), ALU.is_equal)

            def mark_batch(b, slot, part):
                slot2, n = slot % 2, tiles_of(b)
                if part == 0:
                    wait_count(dve, win_ready, b - 1)
                tiles = slice(part * MARK, min((part + 1) * MARK, n))
                if tiles.start >= n:
                    return
                which = rel[:, bass.ds(row_of(b), 1), tiles].rearrange("p o j -> p (o j)").rearrange("p (j o) -> p j o", o=1)
                done = mark(slot2, which, tiles)
                if tiles.stop == n:
                    done.then_inc(onehot_ready, 1)

            def add_window(b, slot):
                base = dve.value_load(base_row[0:1, bass.ds(row_of(b), 1)], min_val=0, max_val=NODES - 1)
                dve.wait_ge(win_ready, b + 1)
                if isinstance(b, int) and b == 0:
                    dve.wait_ge(aggX_cleared, CLEARS)
                wait_count(dve, win_added, b)
                at = aggX[0:SUMS, bass.ds(base, WINDOW)]
                nc.vector.tensor_tensor(at, at, win[slot % 2][0:SUMS, 0:WINDOW], ALU.add).then_inc(win_added, 1)

            def add_rows(s):
                dve.wait_ge(rows_gathered[s.slot], s.use * (16 * POOLED) + 16 * POOLED)
                dve.wait_ge(edges_loaded[s.slot], s.use * 16 + 16)
                to, of = msg[s.slot], rows[s.slot]
                if s.first and s.slot == 0:
                    dve.wait_ge(first_gathered, 16 * (SHORT - POOLED))
                    all_of = slice(0, SHORT * D)
                    nc.vector.tensor_tensor(to[:, all_of], of[:, all_of], to[:, all_of], ALU.add).then_inc(sums_ready, 1)
                else:
                    got, looked_up = slice(0, POOLED * D), slice(POOLED * D, ROW)
                    nc.vector.tensor_tensor(to[:, got], of[:, got], to[:, got], ALU.add).then_inc(sums_step, 1)
                    dve.wait_ge(back_ready, s.b)
                    dve.wait_ge(sums_step, s.b)
                    nc.vector.tensor_tensor(to[:, looked_up], back_ps[:, 0:LOOK * D], to[:, looked_up], ALU.add).then_inc(sums_ready, 1)

            def rest(slot, n, done):
                nc.vector.scalar_tensor_tensor(messages(slot, n), messages(slot, n), 0.0, parts_of(slot, n, 0),
                                               ALU.max, ALU.subtract).then_inc(done, 1)

            def rest_of(b, slot):
                dve.wait_ge(high_ready, b + 1)
                rest(slot, tiles_of(b), rest_ready)

            def low(slot, n, done):
                nc.vector.tensor_tensor(parts_of(slot, n, 2), messages(slot, n), parts_of(slot, n, 1), ALU.subtract).then_inc(done, 1)

            def low_of(b, slot):
                dve.wait_ge(mid_ready, b + 1)
                low(slot, tiles_of(b), msgs_ready)

            def look_up(k, i):
                bl = dve_blocks[i]
                dve.wait_ge(keys_copied, k + 1)
                wait_count(dve, look_used, (k - 1) * BLOCKS + bl + 1)
                nc.vector.tensor_scalar(look[:, bl, :], src_ps[:, :], keys[:, bl:bl + 1], None,
                                        ALU.is_equal).then_inc(look_dve_ready, 1)

            def pick(s):
                dve.wait_ge(side_copied, s.b + 1)
                dve.wait_ge(look_used, s.b * BLOCKS + BLOCKS)
                wait_count(dve, back_ready, s.b)
                nc.vector.scalar_tensor_tensor(picked_sb[:, :], side_sb[:, :], side_of[:, 0:1], found_ps[s.slot % 2][:, :],
                                               ALU.is_equal, ALU.mult).then_inc(picked, 1)

            def batch(s):
                if s.first and s.slot == 0:
                    add_rows(s)
                    for i in range(AHEAD):
                        look_up(0, i)
                if s.looks:
                    for i in range(AHEAD, BY_DVE):
                        look_up(s.b, i)
                        if reaches(s, 1):
                            if i in MARK_AT:
                                mark_batch(s.b - 1, s.slot - 1, MARK_AT.index(i))
                            if i == REST_AT:
                                rest_of(s.b - 1, (s.slot - 1) % RING)
                            if i == LOW_AT:
                                low_of(s.b - 1, (s.slot - 1) % RING)
                        if i == WINDOW_AT and reaches(s, 3):
                            add_window(s.b - 3, s.slot - 3)
                    if s.first and s.slot == 0:
                        find_bases()
                    if s.looks_on:
                        for i in range(AHEAD):
                            look_up(s.b + 1, i)
                    else:
                        for part in range(MARKS):
                            mark_batch(s.b, s.slot, part)
                    pick(s)
                    if s.first and s.slot == 0:
                        place_edges()
                    else:
                        add_rows(s)
                else:
                    add_window(s.b - 3, s.slot - 3)
                    rest_of(s.b - 1, (s.slot - 1) % RING)
                    for part in range(MARKS):
                        mark_batch(s.b, s.slot, part)
                    low_of(s.b - 1, (s.slot - 1) % RING)
                    add_window(s.b - 2, s.slot - 2)
                    add_rows(s)
                    rest_of(s.b, s.slot)
                    add_window(s.b - 1, s.slot - 1)
                    low_of(s.b, s.slot)
                    add_window(s.b, s.slot)

            batches(dve, batch)

            dve.wait_ge(span_ready, 1)
            reach = dve.value_load(span_max[0:1, 0:1], min_val=0, max_val=NODES)
            dve.wait_ge(win_added, BATCHES)
            with dve.If(reach >= WINDOW):
                nc.vector.memset(far[:, :], 0.0).then_inc(far_added, 1)

                def add_far(b, n):
                    relb = rel[:, bass.ds(row_of(b), 1), 0:n].rearrange("p o j -> p (o j)")
                    far_n = far[:, 0:n]
                    dve.wait_ge(far_gathered, row_of(b) * (16 * TILES) + 16 * (SHORT + TILES) if n == TILES else 16 * SHORT)
                    dve.wait_ge(far_loaded, b * 32 + 32)
                    nc.vector.tensor_tensor(msg[0][:, 0:n * D], rows[0][:, 0:n * D], msg[0][:, 0:n * D], ALU.add).then_inc(far_sums, 1)
                    dve.wait_ge(far_high, b + 1)
                    rest(0, n, far_rest)
                    dve.wait_ge(far_mid, b + 1)
                    low(0, n, far_msgs)
                    nc.vector.tensor_scalar(far_n, relb, base_all[:, bass.ds(row_of(b), 1)], 1.0, ALU.add, ALU.add).then_inc(far_step, 1)
                    dve.wait_ge(far_step, b * (WINDOWS + 3) + 1)
                    nc.vector.scalar_tensor_tensor(far_n, relb, float(WINDOW), far_n, ALU.is_ge, ALU.mult).then_inc(far_step, 1)
                    dve.wait_ge(far_step, b * (WINDOWS + 3) + 2)
                    nc.vector.tensor_scalar(far_n, far_n, 1.0, None, ALU.subtract).then_inc(far_step, 1)
                    with dve.Fori(0, WINDOWS) as w:
                        dve.wait_ge(far_step, b * (WINDOWS + 3) + w + 3)
                        mark(0, far_n.rearrange("p (j o) -> p j o", o=1), slice(0, n)).then_inc(far_onehot, 1)
                        dve.wait_ge(far_onehot, b * WINDOWS + w + 1)
                        nc.vector.tensor_scalar(far_n, far_n, float(WINDOW), None, ALU.subtract).then_inc(far_step, 1)
                        dve.wait_ge(far_win, b * WINDOWS + w + 1)
                        at = aggX[0:SUMS, bass.ds(w * WINDOW, WINDOW)]
                        nc.vector.tensor_tensor(at, at, win[0][0:SUMS, 0:WINDOW], ALU.add).then_inc(far_added, 1)

                add_far(0, SHORT)
                with dve.Fori(0, BATCHES - 1) as row:
                    add_far(row + 1, TILES)
                dve.wait_ge(far_added, BATCHES * WINDOWS + 1)
            nc.vector.memset(passes_done[:, :], 0.0).then_inc(agg_ready, 1)

            for k in range(len(ROUNDS_OUT) + 1):
                if k < len(ROUNDS_OUT):
                    t0, per = ROUNDS_OUT[k]
                    dve.wait_ge(sq_ready, k + 1)
                    nc.vector.tensor_reduce(var[:, t0:t0 + per * SIDE].rearrange("p (i r) -> p i r", i=per),
                                            z_round(sq_of(k), per), AX.X, ALU.add).then_inc(var_ready, 1)
                if k >= 1:
                    t0, per = ROUNDS_OUT[k - 1]
                    t = slice(t0, t0 + per * SIDE)
                    dve.wait_ge(std_ready, k)
                    nc.vector.reciprocal(rstd[:, t], rstd[:, t]).then_inc(rstd_ready, 1)
                    dve.wait_ge(rstd_ready, k)
                    nc.vector.tensor_tensor(
                        y_sb[:, t, :].rearrange("p (r i) f -> p i r f", i=per), z_round(z_of(k - 1), per),
                        rstd[:, t].rearrange("p (i r o) -> p i r o", i=per, o=1).to_broadcast([NP, per, SIDE, D]),
                        ALU.mult).then_inc(out_ready, 1)

        @block.scalar
        def _(act):
            act.dma_start(x_sb[:, :, :], x_v).then_inc(x_loaded, 16)
            load_rows(act, dst_b, dst, dst_rows, dst_loaded)
            for r in range(P // D):
                act.dma_start(w_rep[:, r * D:(r + 1) * D], weight).then_inc(weights_loaded, 16)
            act.dma_start(scale[:, :], eps.rearrange("(a b) -> a b", a=1).to_broadcast([P, 1])).then_inc(small_loaded, 16)
            act.dma_start(bias_row[:, :, :], bias.rearrange("(a o f) -> a o f", a=1, o=1).to_broadcast([1, SIDE, D])).then_inc(small_loaded, 16)
            act.dma_start(dst_sb[:, 0:BATCHES - 1, :], dst_v).then_inc(base_all_loaded, 16)
            act.dma_start(dst_sb[:, BATCHES - 1, 0:SHORT], dst_first).then_inc(base_all_loaded, 16)
            for g in range(NT // TGROUP):
                act.wait_ge(xT_ready, g + 1)
                nc.scalar.copy(aggX_v[SUMS:P, g * TGROUP:(g + 1) * TGROUP, :], xT_group(g)).then_inc(x_copied, 1)

            def clear_sums(part):
                if part == 0:
                    act.wait_ge(zeros_ready, 1)
                    act.wait_ge(bases_ready, 1)
                n = PAD // CLEARS
                nc.scalar.copy(aggX[0:SUMS, part * n:(part + 1) * n], zeros[0:SUMS, :].to_broadcast([SUMS, n])).then_inc(aggX_cleared, 1)

            def high_of(b, slot):
                act.wait_ge(sums_ready, b + 1)
                wait_count(act, win_ready, b - 1)
                nc.scalar.activation(parts_of(slot, tiles_of(b), 0), messages(slot, tiles_of(b)), ACT.Relu).then_inc(high_ready, 1)

            def mid_of(b, slot):
                act.wait_ge(rest_ready, b + 1)
                nc.scalar.copy(parts_of(slot, tiles_of(b), 1), messages(slot, tiles_of(b))).then_inc(mid_ready, 1)

            def square(s, i):
                bl = act_blocks[i]
                wait_count(act, look_used, (s.b - 1) * BLOCKS + bl + 1)
                nc.scalar.activation(look[:, bl, :], key_sb[:, :], ACT.Square, bias=minus_keys[:, bl:bl + 1]).then_inc(squared, 1)

            def mark(s, i):
                bl = act_blocks[i]
                act.wait_ge(squared, s.b * BY_ACT + i + 1)
                nc.scalar.activation(look[:, bl, :], look[:, bl, :], ACT.Relu, scale=-2.0, bias=1.0).then_inc(look_act_ready, 1)

            def batch(s):
                if s.looks:
                    act.wait_ge(src_ready, s.b + 1)
                    nc.scalar.copy(key_sb[:, :], src_ps[:, :]).then_inc(keys_copied, 1)
                    act.wait_ge(keys_copied, s.b + 1)
                    square(s, 0)
                    for i in range(BY_ACT):
                        if i + 1 < BY_ACT:
                            square(s, i + 1)
                        mark(s, i)
                        if s.first and s.slot == 1 and i % 3 == 1 and i // 3 < CLEARS:
                            clear_sums(i // 3)
                        if i == HIGH_AT and reaches(s, 1):
                            high_of(s.b - 1, (s.slot - 1) % RING)
                        if i == MID_AT and reaches(s, 1):
                            mid_of(s.b - 1, (s.slot - 1) % RING)
                        if i == COPY_AT:
                            act.wait_ge(side_ready, s.b + 1)
                            wait_count(act, picked, s.b)
                            nc.scalar.copy(side_sb[:, :], side_ps[:, :]).then_inc(side_copied, 1)
                else:
                    high_of(s.b - 1, (s.slot - 1) % RING)
                    mid_of(s.b - 1, (s.slot - 1) % RING)
                    nc.scalar.activation(rstd[:, 0:1], lneps[:, :], ACT.Sqrt)
                    high_of(s.b, s.slot)
                    mid_of(s.b, s.slot)

            batches(act, batch)

            act.wait_ge(span_ready, 1)
            reach = act.value_load(span_max[0:1, 0:1], min_val=0, max_val=NODES)
            with act.If(reach >= WINDOW):
                def split_far(b, n):
                    act.wait_ge(far_sums, b + 1)
                    nc.scalar.activation(parts_of(0, n, 0), messages(0, n), ACT.Relu).then_inc(far_high, 1)
                    act.wait_ge(far_rest, b + 1)
                    nc.scalar.copy(parts_of(0, n, 1), messages(0, n)).then_inc(far_mid, 1)

                split_far(0, SHORT)
                with act.Fori(0, BATCHES - 1) as row:
                    split_far(row + 1, TILES)

            rounds = len(ROUNDS_OUT)
            for k in range(rounds + 2):
                if k < rounds:
                    cols = ROUNDS_OUT[k][1] * NP
                    act.wait_ge(zT_ready, k + 1)
                    if k >= ZRING:
                        act.wait_ge(z_ready, k - ZRING + 1)
                    nc.scalar.activation(zT_sb[k % ZRING][:, 0:cols], zT[k % ZRING][:, 0:cols], ACT.Identity, bias=bias_col[:, 0:1]).then_inc(zT_copied, 1)
                if 1 <= k <= rounds:
                    act.wait_ge(z_ready, k)
                    if k > ZRING:
                        act.wait_ge(var_ready, k - ZRING)
                    nc.scalar.activation(sq_of(k - 1), z_of(k - 1), ACT.Square).then_inc(sq_ready, 1)
                if k >= 2:
                    t0, per = ROUNDS_OUT[k - 2]
                    t = slice(t0, t0 + per * SIDE)
                    act.wait_ge(var_ready, k - 1)
                    nc.scalar.activation(rstd[:, t], var[:, t], ACT.Sqrt, bias=lneps[:, 0:1], scale=1.0 / D).then_inc(std_ready, 1)

        @block.tensor
        def _(pe):
            pe.wait_ge(ident_ready, 1)
            pe.wait_ge(weights_loaded, 16 * (P // D))
            nc.tensor.matmul(back_ps[:, 0:D], w_rep[:, :], ident[0:D, 0:D], start=True, stop=True).then_inc(w_ready, 1)
            pe.wait_ge(bias_ready, 1)
            nc.tensor.matmul(back_ps[:, D:D + 1], bias_row[:, :, :].rearrange("o r f -> o (r f)"), one_one[:, :], start=True, stop=True).then_inc(w_ready, 1)
            pe.wait_ge(x_loaded, 16)
            for g in range(NT // TGROUP):
                if g >= 2:
                    pe.wait_ge(x_copied, g - 1)
                for t in range(TGROUP):
                    last = nc.tensor.transpose(xT[g % 2][0:D, t * NP:(t + 1) * NP], x_sb[:, g * TGROUP + t, :],
                                               ident[0:NP, 0:NP])
                last.then_inc(xT_ready, 1)

            def sum_tiles(slot2, tiles, n):
                for j in tiles:
                    last = nc.tensor.matmul(win[slot2][0:SUMS, 0:WINDOW], msg_parts[slot2][:, j, :, :].rearrange("p n f -> p (n f)"),
                                            onehot[slot2][:, j, :], start=(j == 0), stop=(j == n - 1))
                return last

            def sum_batch(b, slot, part):
                if part == 0:
                    wait_count(pe, win_added, b - 1)
                    pe.wait_ge(onehot_ready, b + 1)
                    pe.wait_ge(msgs_ready, b + 1)
                n = tiles_of(b)
                tiles = range(part * MARK, min((part + 1) * MARK, n))
                if tiles.start >= n:
                    return
                last = sum_tiles(slot % 2, tiles, n)
                if tiles.stop == n:
                    last.then_inc(win_ready, 1)

            def turn_back(s):
                pe.wait_ge(picked, s.b)
                pe.wait_ge(sums_ready, s.b)
                picked_v = picked_sb[:, :].rearrange("r (p j) -> r j p", j=LOOK)
                for j in range(LOOK):
                    last = nc.tensor.matmul(back_ps[:, j * D:(j + 1) * D], picked_v[:, j, :], fold[:, :], start=True, stop=True)
                last.then_inc(back_ready, 1)

            def spread_keys(k, slot2, turns):
                pe.wait_ge(feat_loaded[slot2], turns * 16 + 16)
                wait_count(pe, look_dve_ready, k * BY_DVE)
                wait_count(pe, keys_copied, k)
                nc.tensor.matmul(src_ps[:, :], spread[:, 0, :], feat[slot2][:, :], start=True, stop=True).then_inc(src_ready, 1)

            def look_up(s):
                a = d = 0
                for bl in range(BLOCKS):
                    if bl % SUM_EVERY == 0 and reaches(s, 2):
                        sum_batch(s.b - 2, (s.slot - 2) % RING, bl // SUM_EVERY)
                    if bl == BACK_AT and reaches(s, 1):
                        turn_back(s)
                    if bl == SIDE_AT:
                        wait_count(pe, side_copied, s.b)
                        nc.tensor.matmul(side_ps[:, :], spread[:, 1, :], feat[s.slot % 2][:, :], start=True, stop=True).then_inc(side_ready, 1)
                    if bl == SRC_AT and s.looks_on:
                        spread_keys(s.b + 1, (s.slot + 1) % 2, s.turns + s.slot % 2)
                    if bl == 0:
                        wait_count(pe, picked, s.b - 1)
                    if by_act[bl]:
                        a += 1
                        pe.wait_ge(look_act_ready, s.b * BY_ACT + a)
                    else:
                        d += 1
                        pe.wait_ge(look_dve_ready, s.b * BY_DVE + d)
                    for n in range(PARTS):
                        last = nc.tensor.matmul(found_ps[s.slot % 2][:, :], parts[:, bl, n, :], look[:, bl, :],
                                                start=(bl == 0 and n == 0), stop=(bl == BLOCKS - 1 and n == PARTS - 1))
                    last.then_inc(look_used, 1)

            def batch(s):
                if s.first and s.slot == 0:
                    pe.wait_ge(spread_ready, 1)
                    spread_keys(0, 0, 0)
                    pe.wait_ge(parts_ready, 1)
                    pe.wait_ge(wb_ready, 1)
                    pe.wait_ge(x_copied, NT // TGROUP)
                if s.looks:
                    look_up(s)
                else:
                    turn_back(s)
                    for b in range(BATCHES - 3, BATCHES):
                        for part in range(MARKS):
                            sum_batch(b, b % RING, part)

            batches(pe, batch)

            pe.wait_ge(span_ready, 1)
            reach = pe.value_load(span_max[0:1, 0:1], min_val=0, max_val=NODES)
            with pe.If(reach >= WINDOW):
                def sum_far(b, n):
                    with pe.Fori(0, WINDOWS) as w:
                        pe.wait_ge(far_msgs, b + 1)
                        pe.wait_ge(far_added, b * WINDOWS + w + 1)
                        pe.wait_ge(far_onehot, b * WINDOWS + w + 1)
                        sum_tiles(0, range(n), n).then_inc(far_win, 1)

                sum_far(0, SHORT)
                with pe.Fori(0, BATCHES - 1) as row:
                    sum_far(row + 1, TILES)

            pe.wait_ge(agg_ready, 1)
            for k in range(len(ROUNDS_OUT) + 1):
                if k < len(ROUNDS_OUT):
                    t0, per = ROUNDS_OUT[k]
                    if k >= ZRING:
                        pe.wait_ge(zT_copied, k - ZRING + 1)
                    for r in range(SIDE):
                        last = nc.tensor.matmul(zT[k % ZRING][r * D:(r + 1) * D, 0:per * NP], wb[:, :],
                                                aggX_v[:, t0 + r * per:t0 + (r + 1) * per, :], start=True, stop=True)
                    last.then_inc(zT_ready, 1)
                if k >= 1:
                    per = ROUNDS_OUT[k - 1][1]
                    pe.wait_ge(zT_copied, k)
                    if k > ZRING:
                        pe.wait_ge(out_ready, k - ZRING)
                    for i in range(per):
                        last = nc.tensor.transpose(z[(k - 1) % ZRING][0:NP, i * P:(i + 1) * P], zT_sb[(k - 1) % ZRING][:, i * NP:(i + 1) * NP], ident[:, :])
                    last.then_inc(z_ready, 1)


def kernel(x, src, dst, edge_attr_32, L0_gnn_W, L0_gnn_b, L0_gnn_eps):
    import numpy as np
    import concourse.bacc as bacc
    from concourse import mybir as mb
    from concourse.bass_utils import run_bass_kernel_spmd

    given = {"x": x, "src": src, "dst": dst, "edge": edge_attr_32, "weight": L0_gnn_W, "bias": L0_gnn_b, "eps": L0_gnn_eps}
    arrays = {f"in_{n}": np.ascontiguousarray(a) for n, a in given.items()}
    nc = bacc.Bacc("TRN2", target_bir_lowering=False, num_devices=1)
    args = [nc.dram_tensor(n, a.shape, mb.dt.from_np(a.dtype), kind="ExternalInput").ap() for n, a in arrays.items()]
    out = nc.dram_tensor("out", list(x.shape), mb.dt.float32, kind="ExternalOutput").ap()
    gnn_kernel(nc, *args, out)
    r = run_bass_kernel_spmd(nc, [arrays], core_ids=[0])
    return r.results[0]["out"]
```
